# Optimizing a Trainium2 kernel written in Bass

```python
import numpy as np
import jax
import jax.numpy as jnp

def _softmax(x, axis=-1):
    return jax.nn.softmax(x, axis=axis)

def _gelu(x):
    return jax.nn.gelu(x, approximate=True)

def _silu(x):
    return jax.nn.silu(x)

def _sigmoid(x):
    return jax.nn.sigmoid(x)

def _layernorm(x, axis=-1, eps=1e-05):
    m = jnp.mean(x, axis=axis, keepdims=True)
    v = jnp.var(x, axis=axis, keepdims=True)
    return (x - m) / jnp.sqrt(v + eps)

def _scatter_add(tgt, idx, src, axis=0):
    return tgt.at[idx].add(src)

def _segment_sum(src, seg, n):
    return jax.ops.segment_sum(src, seg, n)
kernel_name = 'mk_hybrid_d2_jaxref_r8_94bdb5'

def setup_inputs(seed: int=0):
    np.random.seed(seed)
    _w = jnp.asarray

    def _L0_attn_a_setup():
        import jax, jax.numpy as jnp
        import numpy as np
        D_MODEL = 128
        N_HEADS = 16
        D_K = D_MODEL // N_HEADS
        MAX_LEN = 256
        B, T = (2, 256)
        key = jax.random.key(seed)
        ks = jax.random.split(key, 10)
        s = 1.0 / np.sqrt(D_MODEL)
        inp = {'x': jax.random.normal(ks[0], (B, T, D_MODEL), dtype=jnp.float32), 'WQ': jax.random.uniform(ks[1], (D_MODEL, D_MODEL), minval=-s, maxval=s, dtype=jnp.float32), 'bQ': jax.random.uniform(ks[2], (D_MODEL,), minval=-s, maxval=s, dtype=jnp.float32), 'WK': jax.random.uniform(ks[3], (D_MODEL, D_MODEL), minval=-s, maxval=s, dtype=jnp.float32), 'bK': jax.random.uniform(ks[4], (D_MODEL,), minval=-s, maxval=s, dtype=jnp.float32), 'WV': jax.random.uniform(ks[5], (D_MODEL, D_MODEL), minval=-s, maxval=s, dtype=jnp.float32), 'bV': jax.random.uniform(ks[6], (D_MODEL,), minval=-s, maxval=s, dtype=jnp.float32), 'WO': jax.random.uniform(ks[7], (D_MODEL, D_MODEL), minval=-s, maxval=s, dtype=jnp.float32), 'bO': jax.random.uniform(ks[8], (D_MODEL,), minval=-s, maxval=s, dtype=jnp.float32), 'rel_pos_table': jax.random.normal(ks[9], (2 * MAX_LEN - 1, N_HEADS), dtype=jnp.float32)}
        return inp
    _L0_attn_a_in = _L0_attn_a_setup()

    def _L0_attn_b_setup():
        import jax, jax.numpy as jnp
        import numpy as np
        from jax import lax
        D_MODEL = 128
        D_STATE = 16
        D_CONV = 4
        EXPAND = 2
        D_INNER = EXPAND * D_MODEL
        DT_RANK = (D_MODEL + 15) // 16
        B, T = (2, 256)

        def _silu(v):
            return v * jax.nn.sigmoid(v)

        def _mamba_forward(x, in_proj_w, conv_w, conv_b, x_proj_w, dt_proj_w, dt_proj_b, A_log, Dp, out_proj_w):
            xz = jnp.einsum('btd,ed->bte', x, in_proj_w)
            xi, z = jnp.split(xz, 2, axis=-1)
            xt = jnp.pad(jnp.transpose(xi, (0, 2, 1)), ((0, 0), (0, 0), (D_CONV - 1, 0)))
            xc = lax.conv_general_dilated(xt, conv_w[:, None, :], window_strides=(1,), padding='VALID', feature_group_count=D_INNER, dimension_numbers=('NCH', 'OIH', 'NCH'))
            xc = _silu(xc + conv_b[None, :, None])
            xc = jnp.transpose(xc, (0, 2, 1))
            x_dbl = jnp.einsum('bti,ei->bte', xc, x_proj_w)
            dt_lo, Bp, Cp = jnp.split(x_dbl, [DT_RANK, DT_RANK + D_STATE], axis=-1)
            dt = jax.nn.softplus(jnp.einsum('btr,ir->bti', dt_lo, dt_proj_w) + dt_proj_b)
            A = -jnp.exp(A_log)
            h0 = jnp.zeros((x.shape[0], D_INNER, D_STATE), dtype=jnp.float32)

            def step(h, inp):
                dt_t, B_t, C_t, x_t = inp
                dA = jnp.exp(dt_t[..., None] * A[None])
                dBx = dt_t[..., None] * B_t[:, None, :] * x_t[..., None]
                h = dA * h + dBx
                y_t = jnp.sum(h * C_t[:, None, :], axis=-1)
                return (h, y_t)
            scan_in = (jnp.moveaxis(dt, 1, 0), jnp.moveaxis(Bp, 1, 0), jnp.moveaxis(Cp, 1, 0), jnp.moveaxis(xc, 1, 0))
            _, ys = lax.scan(step, h0, scan_in)
            y = jnp.moveaxis(ys, 0, 1) + Dp * xc
            y = y * _silu(z)
            return jnp.einsum('bti,di->btd', y, out_proj_w)
        key = jax.random.key(seed)
        ks = jax.random.split(key, 10)
        s = lambda n: 1.0 / np.sqrt(n)
        x = jax.random.normal(ks[0], (B, T, D_MODEL), dtype=jnp.float32)
        in_proj_w = jax.random.uniform(ks[1], (2 * D_INNER, D_MODEL), minval=-s(D_MODEL), maxval=s(D_MODEL))
        conv_w = jax.random.uniform(ks[2], (D_INNER, D_CONV), minval=-s(D_CONV), maxval=s(D_CONV))
        conv_b = jax.random.uniform(ks[3], (D_INNER,), minval=-s(D_CONV), maxval=s(D_CONV))
        x_proj_w = jax.random.uniform(ks[4], (DT_RANK + 2 * D_STATE, D_INNER), minval=-s(D_INNER), maxval=s(D_INNER))
        dt_proj_w = jax.random.uniform(ks[5], (D_INNER, DT_RANK), minval=-s(DT_RANK), maxval=s(DT_RANK))
        dt_proj_b = jax.random.uniform(ks[6], (D_INNER,), minval=-s(DT_RANK), maxval=s(DT_RANK))
        A_log = jnp.log(jnp.tile(jnp.arange(1, D_STATE + 1, dtype=jnp.float32), (D_INNER, 1)))
        Dp = jnp.ones((D_INNER,), dtype=jnp.float32)
        out_proj_w = jax.random.uniform(ks[7], (D_MODEL, D_INNER), minval=-s(D_INNER), maxval=s(D_INNER))
        return {'x': x, 'in_proj_w': in_proj_w, 'conv_w': conv_w, 'conv_b': conv_b, 'x_proj_w': x_proj_w, 'dt_proj_w': dt_proj_w, 'dt_proj_b': dt_proj_b, 'A_log': A_log, 'Dp': Dp, 'out_proj_w': out_proj_w}
    _L0_attn_b_in = _L0_attn_b_setup()

    def _L0_ffn_setup():
        import jax, jax.numpy as jnp
        import numpy as np
        from jax import lax
        T, B, I, M, O = (32, 64, 128, 128, 128)

        def _xavier(key, shape):
            fan_out, fan_in = shape
            limit = float(np.sqrt(6.0 / (fan_in + fan_out)))
            return jax.random.uniform(key, shape, jnp.float32, -limit, limit)
        key = jax.random.key(seed)
        ks = jax.random.split(key, 9)
        x = jax.random.normal(ks[0], (T, B, I), jnp.float32)
        return {'x': x, 'wf': _xavier(ks[1], (M, I)), 'uf': _xavier(ks[2], (M, M)), 'bf': jnp.zeros((M,), jnp.float32), 'wi': _xavier(ks[3], (M, I)), 'ui': _xavier(ks[4], (M, M)), 'bi': jnp.zeros((M,), jnp.float32), 'wc': _xavier(ks[5], (M, I)), 'uc': _xavier(ks[6], (M, M)), 'bc': jnp.zeros((M,), jnp.float32), 'wo': _xavier(ks[7], (O, I)), 'uo': _xavier(ks[8], (O, M)), 'bo': jnp.zeros((O,), jnp.float32), 'in_c': jnp.zeros((M,), jnp.float32)}
    _L0_ffn_in = _L0_ffn_setup()

    def _L1_attn_a_setup():
        import jax, jax.numpy as jnp
        import numpy as np
        DIM = 128
        HEADS = 16
        DIM_HEAD = DIM // HEADS
        LATENT = DIM // 4
        SCALE = DIM_HEAD ** (-0.5)
        key = jax.random.key(seed)
        ks = jax.random.split(key, 8)
        B, S = (2, 256)
        init = lambda k, shape, fan_in: jax.random.normal(k, shape, jnp.float32) * fan_in ** (-0.5)
        return {'x': jax.random.normal(ks[0], (B, S, DIM), jnp.float32), 'Wq': init(ks[1], (DIM, DIM), DIM), 'bq': jnp.zeros((DIM,), jnp.float32), 'Wl': init(ks[2], (DIM, LATENT), DIM), 'bl': jnp.zeros((LATENT,), jnp.float32), 'Wk': init(ks[3], (LATENT, DIM), LATENT), 'bk': jnp.zeros((DIM,), jnp.float32), 'Wv': init(ks[4], (LATENT, DIM), LATENT), 'bv': jnp.zeros((DIM,), jnp.float32), 'Wo': init(ks[5], (DIM, DIM), DIM), 'bo': jnp.zeros((DIM,), jnp.float32)}
    _L1_attn_a_in = _L1_attn_a_setup()

    def _L1_attn_b_setup():
        import jax, jax.numpy as jnp
        import numpy as np
        NUM_HEADS = 16
        THETA = 10000.0

        def _rotate_half(x):
            x = x.reshape(x.shape[:-1] + (-1, 2))
            x1, x2 = (x[..., 0], x[..., 1])
            return jnp.stack((-x2, x1), axis=-1).reshape(x.shape[:-2] + (-1,))

        def _rope(x):
            d_k = x.shape[-1]
            seq_len = x.shape[-2]
            inv_freq = 1.0 / THETA ** (jnp.arange(0, d_k, 2, dtype=jnp.float32) / d_k)
            pos = jnp.arange(seq_len, dtype=jnp.float32)
            theta = pos[:, None] * inv_freq[None, :]
            cos = jnp.repeat(jnp.cos(theta), 2, axis=-1)
            sin = jnp.repeat(jnp.sin(theta), 2, axis=-1)
            return x * cos + _rotate_half(x) * sin
        key = jax.random.key(seed)
        kx, kq, kk, kv, ko = jax.random.split(key, 5)
        B, S, D = (2, 256, 128)
        std = 1.0 / (2.0 * (2 * D) ** 0.5)
        return {'x': jax.random.normal(kx, (B, S, D), dtype=jnp.float32), 'Wq': jax.random.normal(kq, (D, D), dtype=jnp.float32) * std, 'Wk': jax.random.normal(kk, (D, D), dtype=jnp.float32) * std, 'Wv': jax.random.normal(kv, (D, D), dtype=jnp.float32) * std, 'Wo': jax.random.normal(ko, (D, D), dtype=jnp.float32) * std}
    _L1_attn_b_in = _L1_attn_b_setup()

    def _L1_ffn_setup():
        import jax, jax.numpy as jnp
        import numpy as np
        HIDDEN = 128
        NUM_EXPERTS = 8
        TOP_K = 2
        FFN = 512
        BATCH, SEQ = (4, 256)
        key = jax.random.key(seed)
        k_x, k_r, k_w1, k_w2 = jax.random.split(key, 4)
        x = jax.random.normal(k_x, (BATCH, SEQ, HIDDEN), dtype=jnp.float32)
        router_w = jax.random.normal(k_r, (NUM_EXPERTS, HIDDEN), dtype=jnp.float32) * (1.0 / np.sqrt(HIDDEN))
        lim = float(np.sqrt(6.0 / (FFN + HIDDEN)))
        expert_w1 = jax.random.uniform(k_w1, (NUM_EXPERTS, FFN, HIDDEN), dtype=jnp.float32, minval=-lim, maxval=lim)
        expert_w2 = jax.random.uniform(k_w2, (NUM_EXPERTS, HIDDEN, FFN), dtype=jnp.float32, minval=-lim, maxval=lim)
        return {'x': x, 'router_w': router_w, 'expert_w1': expert_w1, 'expert_w2': expert_w2}
    _L1_ffn_in = _L1_ffn_setup()
    _d = {'L0_attn_a_x': _L0_attn_a_in['x'], 'L0_attn_a_WQ': _L0_attn_a_in['WQ'], 'L0_attn_a_bQ': _L0_attn_a_in['bQ'], 'L0_attn_a_WK': _L0_attn_a_in['WK'], 'L0_attn_a_bK': _L0_attn_a_in['bK'], 'L0_attn_a_WV': _L0_attn_a_in['WV'], 'L0_attn_a_bV': _L0_attn_a_in['bV'], 'L0_attn_a_WO': _L0_attn_a_in['WO'], 'L0_attn_a_bO': _L0_attn_a_in['bO'], 'L0_attn_a_rel_pos_table': _L0_attn_a_in['rel_pos_table'], 'L0_attn_b_in_proj_w': _L0_attn_b_in['in_proj_w'], 'L0_attn_b_conv_w': _L0_attn_b_in['conv_w'], 'L0_attn_b_conv_b': _L0_attn_b_in['conv_b'], 'L0_attn_b_x_proj_w': _L0_attn_b_in['x_proj_w'], 'L0_attn_b_dt_proj_w': _L0_attn_b_in['dt_proj_w'], 'L0_attn_b_dt_proj_b': _L0_attn_b_in['dt_proj_b'], 'L0_attn_b_A_log': _L0_attn_b_in['A_log'], 'L0_attn_b_Dp': _L0_attn_b_in['Dp'], 'L0_attn_b_out_proj_w': _L0_attn_b_in['out_proj_w'], 'L0_ffn_wf': _L0_ffn_in['wf'], 'L0_ffn_uf': _L0_ffn_in['uf'], 'L0_ffn_bf': _L0_ffn_in['bf'], 'L0_ffn_wi': _L0_ffn_in['wi'], 'L0_ffn_ui': _L0_ffn_in['ui'], 'L0_ffn_bi': _L0_ffn_in['bi'], 'L0_ffn_wc': _L0_ffn_in['wc'], 'L0_ffn_uc': _L0_ffn_in['uc'], 'L0_ffn_bc': _L0_ffn_in['bc'], 'L0_ffn_wo': _L0_ffn_in['wo'], 'L0_ffn_uo': _L0_ffn_in['uo'], 'L0_ffn_bo': _L0_ffn_in['bo'], 'L0_ffn_in_c': _L0_ffn_in['in_c'], 'L1_attn_a_Wq': _L1_attn_a_in['Wq'], 'L1_attn_a_bq': _L1_attn_a_in['bq'], 'L1_attn_a_Wl': _L1_attn_a_in['Wl'], 'L1_attn_a_bl': _L1_attn_a_in['bl'], 'L1_attn_a_Wk': _L1_attn_a_in['Wk'], 'L1_attn_a_bk': _L1_attn_a_in['bk'], 'L1_attn_a_Wv': _L1_attn_a_in['Wv'], 'L1_attn_a_bv': _L1_attn_a_in['bv'], 'L1_attn_a_Wo': _L1_attn_a_in['Wo'], 'L1_attn_a_bo': _L1_attn_a_in['bo'], 'L1_attn_b_Wq': _L1_attn_b_in['Wq'], 'L1_attn_b_Wk': _L1_attn_b_in['Wk'], 'L1_attn_b_Wv': _L1_attn_b_in['Wv'], 'L1_attn_b_Wo': _L1_attn_b_in['Wo'], 'L1_ffn_router_w': _L1_ffn_in['router_w'], 'L1_ffn_expert_w1': _L1_ffn_in['expert_w1'], 'L1_ffn_expert_w2': _L1_ffn_in['expert_w2']}
    _x0 = _d['L0_attn_a_x']
    _d['L0_attn_a_x'] = jax.random.normal(jax.random.fold_in(jax.random.key(seed), 1), (16, 512, 128), dtype=_x0.dtype)
    del _x0
    return _d

def reference(L0_attn_a_x, L0_attn_a_WQ, L0_attn_a_bQ, L0_attn_a_WK, L0_attn_a_bK, L0_attn_a_WV, L0_attn_a_bV, L0_attn_a_WO, L0_attn_a_bO, L0_attn_a_rel_pos_table, L0_attn_b_in_proj_w, L0_attn_b_conv_w, L0_attn_b_conv_b, L0_attn_b_x_proj_w, L0_attn_b_dt_proj_w, L0_attn_b_dt_proj_b, L0_attn_b_A_log, L0_attn_b_Dp, L0_attn_b_out_proj_w, L0_ffn_wf, L0_ffn_uf, L0_ffn_bf, L0_ffn_wi, L0_ffn_ui, L0_ffn_bi, L0_ffn_wc, L0_ffn_uc, L0_ffn_bc, L0_ffn_wo, L0_ffn_uo, L0_ffn_bo, L0_ffn_in_c, L1_attn_a_Wq, L1_attn_a_bq, L1_attn_a_Wl, L1_attn_a_bl, L1_attn_a_Wk, L1_attn_a_bk, L1_attn_a_Wv, L1_attn_a_bv, L1_attn_a_Wo, L1_attn_a_bo, L1_attn_b_Wq, L1_attn_b_Wk, L1_attn_b_Wv, L1_attn_b_Wo, L1_ffn_router_w, L1_ffn_expert_w1, L1_ffn_expert_w2):

    def _L0_attn_a_ref(x, WQ, bQ, WK, bK, WV, bV, WO, bO, rel_pos_table):
        import jax, jax.numpy as jnp
        import numpy as np
        D_MODEL = 128
        N_HEADS = 16
        D_K = D_MODEL // N_HEADS
        MAX_LEN = 256
        B, T = (2, 256)
        b, t, d = x.shape
        q = (x @ WQ.T + bQ).reshape(b, t, N_HEADS, D_K).transpose(0, 2, 1, 3)
        k = (x @ WK.T + bK).reshape(b, t, N_HEADS, D_K).transpose(0, 2, 1, 3)
        v = (x @ WV.T + bV).reshape(b, t, N_HEADS, D_K).transpose(0, 2, 1, 3)
        scores = jnp.einsum('bhqd,bhkd->bhqk', q, k) / jnp.sqrt(jnp.float32(D_K))
        pos = jnp.arange(t)
        rel = pos[:, None] - pos[None, :] + (MAX_LEN - 1)
        rel = jnp.clip(rel, 0, 2 * MAX_LEN - 2)
        rel_bias = rel_pos_table[rel]
        scores = scores + rel_bias.transpose(2, 0, 1)[None]
        causal = pos[None, :] <= pos[:, None]
        scores = jnp.where(causal[None, None], scores, -jnp.inf)
        attn = jax.nn.softmax(scores, axis=-1)
        out = jnp.einsum('bhqk,bhkd->bhqd', attn, v)
        out = out.transpose(0, 2, 1, 3).reshape(b, t, d)
        return out @ WO.T + bO

    def _L0_attn_b_ref(x, in_proj_w, conv_w, conv_b, x_proj_w, dt_proj_w, dt_proj_b, A_log, Dp, out_proj_w):
        import jax, jax.numpy as jnp
        import numpy as np
        from jax import lax
        D_MODEL = 128
        D_STATE = 16
        D_CONV = 4
        EXPAND = 2
        D_INNER = EXPAND * D_MODEL
        DT_RANK = (D_MODEL + 15) // 16
        B, T = (2, 256)

        def _silu(v):
            return v * jax.nn.sigmoid(v)

        def _mamba_forward(x, in_proj_w, conv_w, conv_b, x_proj_w, dt_proj_w, dt_proj_b, A_log, Dp, out_proj_w):
            xz = jnp.einsum('btd,ed->bte', x, in_proj_w)
            xi, z = jnp.split(xz, 2, axis=-1)
            xt = jnp.pad(jnp.transpose(xi, (0, 2, 1)), ((0, 0), (0, 0), (D_CONV - 1, 0)))
            xc = lax.conv_general_dilated(xt, conv_w[:, None, :], window_strides=(1,), padding='VALID', feature_group_count=D_INNER, dimension_numbers=('NCH', 'OIH', 'NCH'))
            xc = _silu(xc + conv_b[None, :, None])
            xc = jnp.transpose(xc, (0, 2, 1))
            x_dbl = jnp.einsum('bti,ei->bte', xc, x_proj_w)
            dt_lo, Bp, Cp = jnp.split(x_dbl, [DT_RANK, DT_RANK + D_STATE], axis=-1)
            dt = jax.nn.softplus(jnp.einsum('btr,ir->bti', dt_lo, dt_proj_w) + dt_proj_b)
            A = -jnp.exp(A_log)
            h0 = jnp.zeros((x.shape[0], D_INNER, D_STATE), dtype=jnp.float32)

            def step(h, inp):
                dt_t, B_t, C_t, x_t = inp
                dA = jnp.exp(dt_t[..., None] * A[None])
                dBx = dt_t[..., None] * B_t[:, None, :] * x_t[..., None]
                h = dA * h + dBx
                y_t = jnp.sum(h * C_t[:, None, :], axis=-1)
                return (h, y_t)
            scan_in = (jnp.moveaxis(dt, 1, 0), jnp.moveaxis(Bp, 1, 0), jnp.moveaxis(Cp, 1, 0), jnp.moveaxis(xc, 1, 0))
            _, ys = lax.scan(step, h0, scan_in)
            y = jnp.moveaxis(ys, 0, 1) + Dp * xc
            y = y * _silu(z)
            return jnp.einsum('bti,di->btd', y, out_proj_w)
        return _mamba_forward(x, in_proj_w, conv_w, conv_b, x_proj_w, dt_proj_w, dt_proj_b, A_log, Dp, out_proj_w)

    def _L0_ffn_ref(x, wf, uf, bf, wi, ui, bi, wc, uc, bc, wo, uo, bo, in_c):
        import jax, jax.numpy as jnp
        import numpy as np
        from jax import lax
        T, B, I, M, O = (32, 64, 128, 128, 128)

        def _xavier(key, shape):
            fan_out, fan_in = shape
            limit = float(np.sqrt(6.0 / (fan_in + fan_out)))
            return jax.random.uniform(key, shape, jnp.float32, -limit, limit)
        batch = x.shape[1]
        c0 = jnp.broadcast_to(in_c, (batch, in_c.shape[0]))

        def step(c, xt):
            ft = jax.nn.sigmoid(xt @ wf.T + c @ uf.T + bf)
            it = jax.nn.sigmoid(xt @ wi.T + c @ ui.T + bi)
            gt = jnp.tanh(xt @ wc.T + c @ uc.T + bc)
            c = ft * c + it * gt
            return (c, None)
        c_final, _ = lax.scan(step, c0, x)
        h = jnp.tanh(jnp.einsum('tbi,oi->tbo', x, wo) + c_final @ uo.T + bo)
        return h

    def _L1_attn_a_ref(x, Wq, bq, Wl, bl, Wk, bk, Wv, bv, Wo, bo):
        import jax, jax.numpy as jnp
        import numpy as np
        DIM = 128
        HEADS = 16
        DIM_HEAD = DIM // HEADS
        LATENT = DIM // 4
        SCALE = DIM_HEAD ** (-0.5)
        B, S, D = x.shape
        H, Dh = (HEADS, DIM_HEAD)
        q = (x @ Wq + bq).reshape(B, S, H, Dh)
        latent = x @ Wl + bl
        k = (latent @ Wk + bk).reshape(B, S, H, Dh)
        v = (latent @ Wv + bv).reshape(B, S, H, Dh)
        scores = jnp.einsum('bihd,bjhd->bhij', q, k) * SCALE
        attn = jax.nn.softmax(scores, axis=-1)
        out = jnp.einsum('bhij,bjhd->bihd', attn, v).reshape(B, S, D)
        out = out @ Wo + bo
        return out

    def _L1_attn_b_ref(x, Wq, Wk, Wv, Wo):
        import jax, jax.numpy as jnp
        import numpy as np
        NUM_HEADS = 16
        THETA = 10000.0

        def _rotate_half(x):
            x = x.reshape(x.shape[:-1] + (-1, 2))
            x1, x2 = (x[..., 0], x[..., 1])
            return jnp.stack((-x2, x1), axis=-1).reshape(x.shape[:-2] + (-1,))

        def _rope(x):
            d_k = x.shape[-1]
            seq_len = x.shape[-2]
            inv_freq = 1.0 / THETA ** (jnp.arange(0, d_k, 2, dtype=jnp.float32) / d_k)
            pos = jnp.arange(seq_len, dtype=jnp.float32)
            theta = pos[:, None] * inv_freq[None, :]
            cos = jnp.repeat(jnp.cos(theta), 2, axis=-1)
            sin = jnp.repeat(jnp.sin(theta), 2, axis=-1)
            return x * cos + _rotate_half(x) * sin
        B, S, D = x.shape
        H = NUM_HEADS
        d_k = D // H

        def split_heads(t):
            return t.reshape(B, S, H, d_k).transpose(0, 2, 1, 3)
        Q = split_heads(x @ Wq)
        K = split_heads(x @ Wk)
        V = split_heads(x @ Wv)
        Q = _rope(Q)
        K = _rope(K)
        scores = jnp.einsum('bhqd,bhkd->bhqk', Q, K) / jnp.sqrt(jnp.float32(d_k))
        causal = jnp.tril(jnp.ones((S, S), dtype=bool))
        scores = jnp.where(causal[None, None], scores, -jnp.inf)
        attn = jax.nn.softmax(scores, axis=-1)
        out = jnp.einsum('bhqk,bhkd->bhqd', attn, V)
        out = out.transpose(0, 2, 1, 3).reshape(B, S, D)
        return out @ Wo

    def _L1_ffn_ref(x, router_w, expert_w1, expert_w2):
        import jax, jax.numpy as jnp
        import numpy as np
        HIDDEN = 128
        NUM_EXPERTS = 8
        TOP_K = 2
        FFN = 512
        BATCH, SEQ = (4, 256)
        B, S, D = x.shape
        xf = x.reshape(-1, D)
        scores = xf @ router_w.T
        top_v, top_i = jax.lax.top_k(scores, TOP_K)
        routing_w = jax.nn.softmax(top_v, axis=-1)
        out = jnp.zeros_like(xf)
        for e in range(NUM_EXPERTS):
            w_e = jnp.sum(jnp.where(top_i == e, routing_w, 0.0), axis=-1)
            h = jax.nn.gelu(xf @ expert_w1[e].T, approximate=False)
            out = out + h @ expert_w2[e].T * w_e[:, None]
        return out.reshape(B, S, D)
    x = L0_attn_a_x
    x = x + _L0_attn_a_ref(_layernorm(x, axis=-1), L0_attn_a_WQ, L0_attn_a_bQ, L0_attn_a_WK, L0_attn_a_bK, L0_attn_a_WV, L0_attn_a_bV, L0_attn_a_WO, L0_attn_a_bO, L0_attn_a_rel_pos_table)
    x = x + _L0_ffn_ref(_layernorm(x, axis=-1), L0_ffn_wf, L0_ffn_uf, L0_ffn_bf, L0_ffn_wi, L0_ffn_ui, L0_ffn_bi, L0_ffn_wc, L0_ffn_uc, L0_ffn_bc, L0_ffn_wo, L0_ffn_uo, L0_ffn_bo, L0_ffn_in_c)
    x = x + _L0_attn_b_ref(_layernorm(x, axis=-1), L0_attn_b_in_proj_w, L0_attn_b_conv_w, L0_attn_b_conv_b, L0_attn_b_x_proj_w, L0_attn_b_dt_proj_w, L0_attn_b_dt_proj_b, L0_attn_b_A_log, L0_attn_b_Dp, L0_attn_b_out_proj_w)
    x = x + _L0_ffn_ref(_layernorm(x, axis=-1), L0_ffn_wf, L0_ffn_uf, L0_ffn_bf, L0_ffn_wi, L0_ffn_ui, L0_ffn_bi, L0_ffn_wc, L0_ffn_uc, L0_ffn_bc, L0_ffn_wo, L0_ffn_uo, L0_ffn_bo, L0_ffn_in_c)
    x = x + _L1_attn_a_ref(_layernorm(x, axis=-1), L1_attn_a_Wq, L1_attn_a_bq, L1_attn_a_Wl, L1_attn_a_bl, L1_attn_a_Wk, L1_attn_a_bk, L1_attn_a_Wv, L1_attn_a_bv, L1_attn_a_Wo, L1_attn_a_bo)
    x = x + _L1_ffn_ref(_layernorm(x, axis=-1), L1_ffn_router_w, L1_ffn_expert_w1, L1_ffn_expert_w2)
    x = x + _L1_attn_b_ref(_layernorm(x, axis=-1), L1_attn_b_Wq, L1_attn_b_Wk, L1_attn_b_Wv, L1_attn_b_Wo)
    x = x + _L1_ffn_ref(_layernorm(x, axis=-1), L1_ffn_router_w, L1_ffn_expert_w1, L1_ffn_expert_w2)
    return x

_drawn_inputs = setup_inputs


def setup_inputs(seed=0):
    import zlib

    import numpy as np

    out = dict(_drawn_inputs(seed))
    spreads = {'L0_attn_b_Dp': (1.0, 0.6),
     'L0_ffn_bf': (0.0, 0.1),
     'L0_ffn_bi': (0.0, 0.1),
     'L0_ffn_bc': (0.0, 0.1),
     'L0_ffn_bo': (0.0, 0.1),
     'L0_ffn_in_c': (0.0, 0.734),
     'L1_attn_a_bq': (0.0, 0.1),
     'L1_attn_a_bl': (0.0, 0.1),
     'L1_attn_a_bk': (0.0, 0.8),
     'L1_attn_a_bv': (0.0, 0.1),
     'L1_attn_a_bo': (0.0, 0.1)}
    factors = {'L0_attn_a_bQ': 6.782,
     'L0_attn_a_bK': 8.0,
     'L0_attn_b_x_proj_w': 6.744,
     'L0_attn_b_dt_proj_w': 8.0,
     'L0_attn_b_dt_proj_b': 8.0,
     'L0_attn_b_A_log': 8.0,
     'L1_attn_b_Wq': 8.0,
     'L1_attn_b_Wk': 8.0,
     'L1_attn_b_Wv': 2.738}
    for name, (base, spread) in spreads.items():
        noise = np.random.default_rng([zlib.crc32(name.encode()), seed]).standard_normal(out[name].shape)
        drawn = base * np.exp(spread * noise) if base else spread * noise
        out[name] = jnp.asarray(drawn.astype(out[name].dtype))
    for name, factor in factors.items():
        out[name] = (out[name] * factor).astype(out[name].dtype)
    return out
```

```python
from contextlib import ExitStack

import concourse.bass as bass
from concourse import mybir

F32 = mybir.dt.float32
BF16 = mybir.dt.bfloat16
ds = bass.ds
ALU = mybir.AluOpType
ACT = mybir.ActivationFunctionType
X = mybir.AxisListType.X

P = 128
NB = 16
T = 512
NTOK = NB * T
HEADS, DK = 16, 8
EPS = 1e-5


class Core:

    def __init__(self, nc, ctx):
        self.nc, self.ctx, self.serial = nc, ctx, 0

    def phase(self):
        self.serial += 1
        return Phase(self.nc, f"p{self.serial}_")


class Phase:

    def __init__(self, nc, prefix):
        self.nc, self.prefix, self.ctx, self.sems = nc, prefix, ExitStack(), []

    def __enter__(self):
        self.ctx.__enter__()
        return self

    def __exit__(self, *a):
        self.ctx.__exit__(*a)
        if a[0] is None:
            self.nc.clear_and_free_semaphores(self.sems)
            self.nc.all_engine_barrier()

    def sb(self, name, shape, dt=F32):
        return self.ctx.enter_context(self.nc.sbuf_tensor(self.prefix + name, shape, dt))

    def ps(self, name, shape, dt=F32):
        return self.ctx.enter_context(self.nc.psum_tensor(self.prefix + name, shape, dt))

    def sem(self, name):
        self.sems.append(self.nc.alloc_semaphore(self.prefix + name))
        return self.sems[-1]

    def block(self):
        return self.ctx.enter_context(self.nc.Block())


def tok(buf, n, size=T):
    return buf[:, ds(n * size, size)]


def load_x(core, x_dram, x, ident, constant_loads):
    D = 4
    xd = x_dram.rearrange("b (c p) d -> b p c d", p=P)
    with core.phase() as ph:
        stage = ph.sb("stage", [P, D, 4, P])
        turned_ps = ph.ps("turned_ps", [P, D, T])
        constants = ph.sem("constants_loaded")
        constants_behind = ph.sem("constants_behind")
        staged = [ph.sem(f"staged{u}") for u in range(D)]
        turned = ph.sem("turned")
        copied = ph.sem("copied")
        ident_loaded = ph.sem("ident_loaded")
        block = ph.block()

        @block.sync
        def _(sp):
            sp.dma_start(ident[0][:, :], ident[1]).then_inc(ident_loaded, 16)
            with sp.Fori(0, NB // D) as i:
                for u in range(D):
                    sp.wait_ge(turned, D * i + u + 1)
                    sp.dma_start(stage[:, u], xd[ds(D * i + u, 1)].rearrange("a p c d -> (a p) c d")
                                 ).then_inc(staged[u], 16)
            for dst, src in constant_loads[1::3]:
                sp.dma_start(dst, src).then_inc(constants_behind, 16)
            sp.wait_ge(constants_behind, 16 * len(constant_loads[1::3]))

        @block.gpsimd
        def _(pool):
            for i, (dst, src) in enumerate(constant_loads):
                if i % 3 != 1:
                    pool.dma_start(dst, src).then_inc(constants, 16)
            pool.wait_ge(constants, 16 * (len(constant_loads) - len(constant_loads[1::3])))

        @block.tensor
        def _(pe):
            pe.sem_inc(turned, D)
            pe.wait_ge(ident_loaded, 16)
            with pe.Fori(0, NB // D) as i:
                for u in range(D):
                    pe.wait_ge(staged[u], 16 * i + 16)
                    pe.wait_ge(copied, D * i + u + 1)
                    for c in range(4):
                        last = pe.transpose(turned_ps[:, u, c * P:(c + 1) * P], stage[:, u, c], ident[0][:, :])
                    last.then_inc(turned, 1)

        @block.scalar
        def _(act):
            act.sem_inc(copied, D)
            with act.Fori(0, NB // D) as i:
                for u in range(D):
                    act.wait_ge(turned, D + D * i + u + 1)
                    act.activation(tok(x, D * i + u), turned_ps[:, u], ACT.Copy).then_inc(copied, 1)


def store_x(core, out_dram, x, ident):
    D = 4
    od = out_dram.rearrange("b (c p) d -> b p c d", p=P)
    with core.phase() as ph:
        stage = ph.sb("stage", [P, D, 4, P])
        result = ph.sb("result", [P, D, 4, P])
        turned_ps = ph.ps("turned_ps", [P, D, T])
        staged = ph.sem("staged")
        turned = ph.sem("turned")
        copied = ph.sem("copied")
        stored = [ph.sem(f"stored{u}") for u in range(D)]
        block = ph.block()

        @block.scalar
        def _(act):
            with act.Fori(0, NB // D) as i:
                for u in range(D):
                    act.wait_ge(turned, D * i + u + 1)
                    act.activation(stage[:, u].rearrange("p c d -> p (c d)"), tok(x, D * i + u), ACT.Copy
                                   ).then_inc(staged, 1)

        @block.tensor
        def _(pe):
            pe.sem_inc(turned, D)
            with pe.Fori(0, NB // D) as i:
                for u in range(D):
                    pe.wait_ge(staged, D * i + u + 1)
                    pe.wait_ge(copied, D * i + u + 1)
                    for c in range(4):
                        last = pe.transpose(turned_ps[:, u, c * P:(c + 1) * P], stage[:, u, c], ident[:, :])
                    last.then_inc(turned, 1)

        @block.vector
        def _(dve):
            dve.sem_inc(copied, D)
            with dve.Fori(0, NB // D) as i:
                for u in range(D):
                    dve.wait_ge(turned, D + D * i + u + 1)
                    dve.wait_ge(stored[u], 16 * i + 16)
                    dve.tensor_copy(result[:, u].rearrange("p c d -> p (c d)"), turned_ps[:, u]).then_inc(copied, 1)

        @block.sync
        def _(sp):
            for u in range(D):
                sp.sem_inc(stored[u], 16)
            with sp.Fori(0, NB // D) as i:
                for u in range(D):
                    sp.wait_ge(copied, D + D * i + u + 1)
                    sp.dma_start(od[ds(D * i + u, 1)].rearrange("a p c d -> (a p) c d"), result[:, u]
                                 ).then_inc(stored[u], 16)
            for u in range(D):
                sp.wait_ge(stored[u], 16 * (NB // D) + 16)


def layer_norm(core, x, xn, mean_mat, eps):
    D, W = 2, 2 * T
    with core.phase() as ph:
        mean_ps, var_ps = ph.ps("mean_ps", [P, D, W]), ph.ps("var_ps", [P, D, W])
        cen, square, rstd = ph.sb("cen", [P, D, W]), ph.sb("square", [P, D, W]), ph.sb("rstd", [P, D, W])
        mean_ready = ph.sem("mean_ready")
        centred = ph.sem("centred")
        squared = ph.sem("squared")
        var_ready = ph.sem("var_ready")
        log_ready = ph.sem("log_ready")
        rstd_ready = ph.sem("rstd_ready")
        normed = ph.sem("normed")
        block = ph.block()

        @block.tensor
        def _(pe):
            pe.sem_inc(var_ready, D)
            with pe.Fori(0, NTOK // W // D) as i:
                for u in range(D):
                    n = D * i + u
                    pe.wait_ge(centred, n + 1)
                    for c in range(2):
                        last = pe.matmul(mean_ps[:, u, c * T:(c + 1) * T], mean_mat[:, :], tok(x, 2 * n + c),
                                         start=True, stop=True)
                    last.then_inc(mean_ready, 1)
                for u in range(D):
                    n = D * i + u
                    pe.wait_ge(squared, n + 1)
                    pe.wait_ge(log_ready, n + 1)
                    for c in range(2):
                        last = pe.matmul(var_ps[:, u, c * T:(c + 1) * T], mean_mat[:, :],
                                         square[:, u, c * T:(c + 1) * T], start=True, stop=True)
                    last.then_inc(var_ready, 1)

        @block.vector
        def _(dve):
            dve.sem_inc(centred, D)
            with dve.Fori(0, NTOK // W // D) as i:
                for u in range(D):
                    n = D * i + u
                    dve.wait_ge(mean_ready, n + 1)
                    dve.wait_ge(normed, n + 1)
                    dve.tensor_tensor(cen[:, u], tok(x, n, W), mean_ps[:, u], ALU.subtract).then_inc(centred, 1)

        @block.scalar
        def _(act):
            act.sem_inc(log_ready, D)
            act.preload_act_table_set("natural_log_exp_and_others")
            with act.Fori(0, NTOK // W // D) as i:
                for u in range(D):
                    n = D * i + u
                    act.wait_ge(centred, D + n + 1)
                    act.wait_ge(var_ready, n + 1)
                    act.activation(square[:, u], cen[:, u], ACT.Square).then_inc(squared, 1)
                for u in range(D):
                    n = D * i + u
                    act.wait_ge(var_ready, D + n + 1)
                    act.wait_ge(normed, n + 1)
                    act.activation(rstd[:, u], var_ps[:, u], ACT.Ln, bias=eps[:, 0:1]).then_inc(log_ready, 1)
                    act.wait_ge(log_ready, D + n + 1)
                    act.activation(rstd[:, u], rstd[:, u], ACT.Exp, scale=-0.5).then_inc(rstd_ready, 1)

        @block.gpsimd
        def _(pool):
            pool.sem_inc(normed, D)
            with pool.Fori(0, NTOK // W // D) as i:
                for u in range(D):
                    n = D * i + u
                    pool.wait_ge(rstd_ready, n + 1)
                    pool.tensor_tensor(tok(xn, n, W), cen[:, u], rstd[:, u], ALU.mult).then_inc(normed, 1)


def recurrent_ffn(core, x, xn, w, bias):
    H = T // 2
    G = 3
    with core.phase() as ph:
        gate_ps = ph.ps("gate_ps", [P, 2 * G, T])
        out_ps = ph.ps("out_ps", [P, 2, T])
        gate = ph.sb("gate", [P, 2 * G, H])
        kept, added = ph.sb("kept", [P, 2, H]), ph.sb("added", [P, 2, H])
        c = ph.sb("c", [P, 2 * H])
        from_c = ph.sb("from_c", [P, T])
        pre, act_out = ph.sb("pre", [P, 2, T]), ph.sb("act_out", [P, 2, T])
        products = ph.sem("products")
        gated = ph.sem("gated")
        partial = ph.sem("partial")
        c_ready = ph.sem("c_ready")
        zeroed = ph.sem("zeroed")
        uo_ready = ph.sem("uo_ready")
        from_c_ready = ph.sem("from_c_ready")
        wo_ready = ph.sem("wo_ready")
        pre_ready = ph.sem("pre_ready")
        h_ready = ph.sem("h_ready")
        h_added = ph.sem("h_added")
        block = ph.block()

        @block.tensor
        def _(pe):
            with pe.Fori(0, NB) as t:
                for h in range(2):
                    for g in range(G):
                        n = (2 * t + h) * G + g
                        pe.wait_ge(gated, n + 1)
                        pe.matmul(gate_ps[:, h * G + g, 0:H], w[:, 2 * g], tok(xn, 2 * t + h, H),
                                  start=True, stop=False)
                    pe.wait_ge(c_ready, 2 * t + h + 1)
                    for g in range(G):
                        pe.matmul(gate_ps[:, h * G + g, 0:H], w[:, 2 * g + 1], c[:, h * H:(h + 1) * H],
                                  start=False, stop=True).then_inc(products, 1)
            pe.wait_ge(c_ready, 2 * NB + 2)
            pe.matmul(out_ps[:, 0], w[:, 7], c[:, :], start=True, stop=True).then_inc(uo_ready, 1)
            pe.wait_ge(from_c_ready, 1)
            with pe.Fori(0, NB // 2) as i:
                for u in range(2):
                    pe.wait_ge(pre_ready, 2 * i + u + 1)
                    pe.matmul(out_ps[:, u], w[:, 6], tok(xn, 2 * i + u), start=True, stop=True
                              ).then_inc(wo_ready, 1)

        @block.scalar
        def _(act):
            act.sem_inc(gated, 2 * G)
            act.sem_inc(h_ready, 2)
            with act.Fori(0, NB) as t:
                for h in range(2):
                    act.wait_ge(c_ready, 2 * t + h + 1)
                    for g in range(G):
                        act.wait_ge(products, (2 * t + h) * G + g + 1)
                        act.activation(gate[:, h * G + g], gate_ps[:, h * G + g, 0:H],
                                       ACT.Tanh if g == 2 else ACT.Sigmoid, bias=bias[:, g:g + 1]
                                       ).then_inc(gated, 1)
            with act.Fori(0, NB // 2) as i:
                for u in range(2):
                    act.wait_ge(pre_ready, 2 + 2 * i + u + 1)
                    act.wait_ge(h_added, 2 * i + u + 1)
                    act.activation(act_out[:, u], pre[:, u], ACT.Tanh, bias=bias[:, 3:4]).then_inc(h_ready, 1)

        @block.vector
        def _(dve):
            dve.sem_inc(pre_ready, 2)
            dve.memset(c[:, :], 0.0).then_inc(zeroed, 1)
            dve.wait_ge(zeroed, 1)
            for h in range(2):
                dve.tensor_scalar(c[:, h * H:(h + 1) * H], c[:, h * H:(h + 1) * H], bias[:, 4:5], None, ALU.add
                                  ).then_inc(c_ready, 1)
            with dve.Fori(0, NB) as t:
                for h in range(2):
                    ch = c[:, h * H:(h + 1) * H]
                    dve.wait_ge(gated, 2 * G + (2 * t + h) * G + 1)
                    dve.wait_ge(c_ready, 2 * t + h + 1)
                    dve.tensor_tensor(kept[:, h], gate[:, h * G], ch, ALU.mult).then_inc(partial, 1)
                    dve.wait_ge(gated, 2 * G + (2 * t + h) * G + 3)
                    dve.tensor_tensor(added[:, h], gate[:, h * G + 1], gate[:, h * G + 2], ALU.mult
                                      ).then_inc(partial, 1)
                    dve.wait_ge(partial, 2 * (2 * t + h) + 2)
                    dve.tensor_tensor(ch, kept[:, h], added[:, h], ALU.add).then_inc(c_ready, 1)
            dve.wait_ge(uo_ready, 1)
            dve.tensor_copy(from_c[:, :], out_ps[:, 0]).then_inc(from_c_ready, 1)
            dve.wait_ge(from_c_ready, 1)
            with dve.Fori(0, NB // 2) as i:
                for u in range(2):
                    dve.wait_ge(wo_ready, 2 * i + u + 1)
                    dve.wait_ge(h_ready, 2 * i + u + 1)
                    dve.tensor_tensor(pre[:, u], from_c[:, :], out_ps[:, u], ALU.add).then_inc(pre_ready, 1)

        @block.gpsimd
        def _(pool):
            pool.sem_inc(h_added, 2)
            with pool.Fori(0, NB // 2) as i:
                for u in range(2):
                    pool.wait_ge(h_ready, 2 + 2 * i + u + 1)
                    pool.tensor_tensor(tok(x, 2 * i + u), tok(x, 2 * i + u), act_out[:, u], ALU.add
                                       ).then_inc(h_added, 1)


E, FFN = 8, 512
FC = FFN // P


def experts(core, x, xn, w1_dram, w2_dram, route_dram, router, earlier, ident):
    NT = NTOK // P
    with core.phase() as ph:
        w1, w2 = ph.sb("w1", [P, E, FFN]), ph.sb("w2", [P, E, FC, P])
        w_loaded = [ph.sem(f"w_loaded{e}") for e in range(E)]
        with core.phase() as rp:
            xs = rp.sb("xs", [P, 2, T])
            logits = rp.sb("logits", [P, NT, E])
            ahead, equal = rp.sb("ahead", [P, NT, E, E]), rp.sb("equal", [P, NT, E, E])
            rank, chosen, prob = rp.sb("rank", [P, NT, E]), rp.sb("chosen", [P, NT, E]), rp.sb("prob", [P, NT, E])
            top, total, inv = rp.sb("top", [P, NT]), rp.sb("total", [P, NT]), rp.sb("inv", [P, NT])
            route_sb = rp.sb("route_sb", [P, 4, P])
            logit_ps = rp.ps("logit_ps", [P, 2, T])
            route_ps = rp.ps("route_ps", [P, 4, P])
            fixed, scored, logit_ready = rp.sem("fixed"), rp.sem("scored"), rp.sem("logit_ready")
            step = rp.sem("step")
            centred, prob_ready, weight_ready = rp.sem("centred"), rp.sem("prob_ready"), rp.sem("weight_ready")
            turned, turned_out, stored = rp.sem("turned"), rp.sem("turned_out"), rp.sem("stored")
            block = rp.block()

            @block.scalar
            def _(act):
                with act.Fori(0, NB // 2) as i:
                    for u in range(2):
                        act.wait_ge(scored, 2 * i + u + 1)
                        act.activation(xs[:, u], tok(xn, 2 * i + u), ACT.Copy).then_inc(fixed, 1)
                act.wait_ge(centred, 1)
                act.activation(prob[:, :, :], prob[:, :, :], ACT.Exp).then_inc(prob_ready, 1)
                act.wait_ge(turned, 1)
                act.activation(route_sb[:, :, :], route_ps[:, :, :], ACT.Copy).then_inc(turned_out, 1)

            @block.tensor
            def _(pe):
                pe.sem_inc(scored, 2)
                with pe.Fori(0, NB // 2) as i:
                    for u in range(2):
                        pe.wait_ge(fixed, 2 * i + u + 1)
                        pe.wait_ge(logit_ready, 2 * i + u + 1)
                        for c in range(4):
                            last = pe.matmul(logit_ps[:, u, c * E:(c + 1) * E], xs[:, u, c * P:(c + 1) * P],
                                             router[:, :], start=True, stop=True)
                        last.then_inc(scored, 1)
                pe.wait_ge(weight_ready, 1)
                for q in range(4):
                    last = pe.transpose(route_ps[:, q], prob[:, 16 * q:16 * q + 16, :].rearrange("p a b -> p (a b)"),
                                        ident[:, :])
                last.then_inc(turned, 1)

            @block.vector
            def _(dve):
                dve.sem_inc(logit_ready, 2)
                with dve.Fori(0, NB // 2) as i:
                    for u in range(2):
                        dve.wait_ge(scored, 2 + 2 * i + u + 1)
                        dve.tensor_copy(logits[:, ds(4 * (2 * i + u), 4), :],
                                        logit_ps[:, u, 0:4 * E].rearrange("p (a b) -> p a b", b=E)
                                        ).then_inc(logit_ready, 1)
                dve.wait_ge(logit_ready, 2 + NB)
                mine = logits[:, :, :].unsqueeze(3).to_broadcast([P, NT, E, E])
                others = logits[:, :, :].unsqueeze(2).to_broadcast([P, NT, E, E])
                dve.tensor_tensor(ahead[:, :, :, :], others, mine, ALU.is_gt).then_inc(step, 1)
                dve.tensor_tensor(equal[:, :, :, :], others, mine, ALU.is_equal).then_inc(step, 1)
                dve.tensor_reduce(top[:, :], logits[:, :, :], X, ALU.max).then_inc(step, 1)
                dve.wait_ge(step, 3)
                dve.tensor_tensor(prob[:, :, :], logits[:, :, :], top[:, :].unsqueeze(2).to_broadcast([P, NT, E]),
                                  ALU.subtract).then_inc(centred, 1)
                dve.tensor_tensor(equal[:, :, :, :], equal[:, :, :, :],
                                  earlier[:, :, :].unsqueeze(1).to_broadcast([P, NT, E, E]), ALU.mult).then_inc(step, 1)
                dve.wait_ge(step, 4)
                dve.tensor_tensor(ahead[:, :, :, :], ahead[:, :, :, :], equal[:, :, :, :], ALU.add).then_inc(step, 1)
                dve.wait_ge(step, 5)
                dve.tensor_reduce(rank[:, :, :], ahead[:, :, :, :], X, ALU.add).then_inc(step, 1)
                dve.wait_ge(step, 6)
                dve.tensor_scalar(chosen[:, :, :], rank[:, :, :], 2.0, None, ALU.is_lt).then_inc(step, 1)
                dve.wait_ge(step, 7)
                dve.wait_ge(prob_ready, 1)
                dve.tensor_tensor(prob[:, :, :], prob[:, :, :], chosen[:, :, :], ALU.mult).then_inc(step, 1)
                dve.wait_ge(step, 8)
                dve.tensor_reduce(total[:, :], prob[:, :, :], X, ALU.add).then_inc(step, 1)
                dve.wait_ge(step, 9)
                dve.reciprocal(inv[:, :], total[:, :]).then_inc(step, 1)
                dve.wait_ge(step, 10)
                dve.tensor_tensor(prob[:, :, :], prob[:, :, :], inv[:, :].unsqueeze(2).to_broadcast([P, NT, E]),
                                  ALU.mult).then_inc(weight_ready, 1)

            @block.sync
            def _(sp):
                for e in range(E):
                    sp.dma_start(w1[:, e], w1_dram[:, e]).then_inc(w_loaded[e], 16)
                    sp.dma_start(w2[:, e], w2_dram[:, e]).then_inc(w_loaded[e], 16)
                sp.wait_ge(turned_out, 1)
                sp.dma_start(route_dram.rearrange("q p c -> p q c"), route_sb[:, :, :]).then_inc(stored, 16)
                sp.wait_ge(stored, 16)

        with core.phase() as mp:
            route = mp.sb("route", [P, 2, 4, E, P])
            hidden = mp.sb("hidden", [P, 2, FC, T])
            weighted = mp.sb("weighted", [P, 2, T])
            hid_ps = mp.ps("hid_ps", [P, FC, T])
            out_ps = mp.ps("out_ps", [P, 2, T])
            routed = [mp.sem(f"routed{u}") for u in range(2)]
            hid_mm = mp.sem("hid_mm")
            gelu = mp.sem("gelu")
            out_mm = mp.sem("out_mm")
            weigh = mp.sem("weigh")
            CREDITS = E + 2
            summed = mp.sem("summed")
            block = mp.block()
            route_chunks = route_dram.rearrange("q (s r) c -> (q s) (r c)", s=4)

            @block.sync
            def _(sp):
                with sp.Fori(0, NB // 2) as i:
                    for u in range(2):
                        sp.wait_ge(weigh, CREDITS + E * (2 * i + u - 1))
                        sp.dma_start(route[:, u].rearrange("p t e c -> p (t e c)"),
                                     route_chunks[ds(2 * i + u, 1)].to_broadcast([P, 4 * E * P])
                                     ).then_inc(routed[u], 16)

            @block.tensor
            def _(pe):
                pe.sem_inc(out_mm, 2)
                for e in range(E):
                    pe.wait_ge(w_loaded[e], 32)

                def up(b, e, f):
                    pe.wait_ge(gelu, (b * E + e) * FC + f + 1)
                    pe.matmul(hid_ps[:, f], w1[:, e, f * P:(f + 1) * P], tok(xn, b), start=True, stop=True
                              ).then_inc(hid_mm, 1)

                def down(b, e, f):
                    if f == 0:
                        pe.wait_ge(weigh, CREDITS - 1 + b * E + e)
                    pe.wait_ge(gelu, FC + (b * E + e) * FC + f + 1)
                    mm = pe.matmul(out_ps[:, e % 2], w2[:, e, f], hidden[:, e % 2, f],
                                   start=(f == 0), stop=(f == FC - 1))
                    if f == FC - 1:
                        mm.then_inc(out_mm, 1)

                with pe.Fori(0, NB) as b:
                    for f in range(FC):
                        up(b, 0, f)
                    for e in range(E):
                        for f in range(FC):
                            if e + 1 < E:
                                up(b, e + 1, f)
                            down(b, e, f)

            @block.scalar
            def _(act):
                act.sem_inc(gelu, FC)
                with act.Fori(0, NB) as b:
                    for e in range(E):
                        act.wait_ge(out_mm, b * E + e + 1)
                        for f in range(FC):
                            act.wait_ge(hid_mm, (b * E + e) * FC + f + 1)
                            act.activation(hidden[:, e % 2, f], hid_ps[:, f], ACT.Gelu).then_inc(gelu, 1)

            @block.vector
            def _(dve):
                dve.sem_inc(weigh, CREDITS)
                dve.sem_inc(summed, 2)
                with dve.Fori(0, NB // 2) as i:
                    for u in range(2):
                        dve.wait_ge(routed[u], 16 * i + 16)
                        for e in range(E):
                            n = (2 * i + u) * E + e
                            dve.wait_ge(out_mm, 2 + n + 1)
                            dve.wait_ge(summed, n + 1)
                            dve.tensor_tensor(weighted[:, e % 2].rearrange("p (t c) -> p t c", c=P), route[:, u, :, e],
                                              out_ps[:, e % 2].rearrange("p (t c) -> p t c", c=P), ALU.mult
                                              ).then_inc(weigh, 1)
                            dve.wait_ge(weigh, CREDITS + n + 1)
                            dve.wait_ge(summed, 2 + n)
                            dve.tensor_tensor(tok(x, 2 * i + u), tok(x, 2 * i + u), weighted[:, e % 2], ALU.add
                                              ).then_inc(summed, 1)


Q_PARTS = (0, 0, 0, 1, 1, 2)
K_PARTS = (0, 1, 2, 0, 1, 0)
STEPS = ((0, 3), (3, 2), (5, 1))
PLACES = len(Q_PARTS)
ROWS = PLACES * DK
SHIFT_ROWS = 2
MASKED = -1e30


def project(core, x_n, stacks, v_dram, w):
    latent, rotary = "wl" in w, "cos" in w
    C = 32 if latent else P
    with core.phase() as ph:
        xs = ph.sb("xs", [C, 2, T])
        whole = ph.sb("whole", [P, 2, 2, T])
        rest = ph.sb("rest", [P, 2, 2, T])
        parts = ph.sb("parts", [P, 3, 2, 2, T], BF16)
        v_sb = ph.sb("v_sb", [P, 2, 4, P])
        if rotary:
            by_cos, by_sin = ph.sb("by_cos", [P, 2, T]), ph.sb("by_sin", [P, 2, T])
        side_ps = ph.ps("side_ps", [P, 2, 2, T])
        v_ps = ph.ps("v_ps", [P, 2, T])
        lat_ps = ph.ps("lat_ps", [P, T])
        lat_mm = ph.sem("lat_mm")
        fixed = ph.sem("fixed")
        side_mm = ph.sem("side_mm")
        v_mm = ph.sem("v_mm")
        whole_ready = ph.sem("whole_ready")
        turned_ready = ph.sem("turned_ready")
        rest_ready = ph.sem("rest_ready")
        cast = ph.sem("cast")
        low_ready = ph.sem("low_ready")
        v_ready = ph.sem("v_ready")
        stored = [ph.sem(f"stored{u}") for u in range(2)]
        STORES = 2 * len(STEPS) + 1
        block = ph.block()

        @block.tensor
        def _(pe):
            pe.sem_inc(v_mm, 2)
            with pe.Fori(0, NB // 2) as i:
                for u in range(2):
                    n = 2 * i + u
                    if latent:
                        pe.wait_ge(fixed, n + 1)
                        pe.matmul(lat_ps[0:C, :], w["wl"], tok(x_n, n), start=True, stop=True).then_inc(lat_mm, 1)
                    for s, name in enumerate(("wq", "wk")):
                        src = xs[:, u] if latent and s == 1 else tok(x_n, n)
                        if latent and s == 1:
                            pe.wait_ge(fixed, 1 + n + 1)
                        pe.wait_ge(whole_ready, 2 * n + s + 1)
                        mm = pe.matmul(side_ps[:, s, 0], w[name], src, start=True, stop=True)
                        if rotary:
                            mm = pe.matmul(side_ps[:, s, 1], w[name + "_turned"], src, start=True, stop=True)
                        mm.then_inc(side_mm, 1)
                    pe.wait_ge(fixed, 1 + n + 1)
                    pe.wait_ge(v_ready, n + 1)
                    for c in range(4):
                        mm = pe.matmul(v_ps[:, u, c * P:(c + 1) * P], xs[:, u, c * P:(c + 1) * P], w["wv"],
                                       start=True, stop=True)
                    mm.then_inc(v_mm, 1)

        @block.scalar
        def _(act):
            act.sem_inc(fixed, 1)
            if not rotary:
                act.sem_inc(whole_ready, 2)
            with act.Fori(0, NB // 2) as i:
                for u in range(2):
                    n = 2 * i + u
                    act.wait_ge(v_mm, n + 1)
                    if latent:
                        act.wait_ge(lat_mm, n + 1)
                        act.activation(xs[:, u], lat_ps[0:C, :], ACT.Identity, bias=w["bl"]).then_inc(fixed, 1)
                    else:
                        act.activation(xs[:, u], tok(x_n, n), ACT.Copy).then_inc(fixed, 1)
                    act.wait_ge(stored[u], 16 * STORES * (i + 1))
                    for s, bias in enumerate(("bq", "bk")):
                        if not rotary:
                            act.wait_ge(side_mm, 2 * n + s + 1)
                            act.wait_ge(rest_ready, 2 * n + s + 1)
                            act.activation(whole[:, s, u], side_ps[:, s, 0], ACT.Identity, bias=w[bias]
                                           ).then_inc(whole_ready, 1)
                        act.wait_ge(whole_ready, 2 + 2 * n + s + 1)
                        act.activation(parts[:, 0, s, u], whole[:, s, u], ACT.Copy).then_inc(cast, 1)
                    for s in range(2):
                        act.wait_ge(rest_ready, 4 + 2 * n + s + 1)
                        act.activation(parts[:, 1, s, u], rest[:, s, u], ACT.Copy).then_inc(cast, 1)

        @block.vector
        def _(dve):
            dve.sem_inc(rest_ready, 4)
            dve.sem_inc(v_ready, 2)
            with dve.Fori(0, NB // 2) as i:
                for u in range(2):
                    n = 2 * i + u
                    for s in range(2):
                        if rotary:
                            dve.wait_ge(side_mm, 2 * n + s + 1)
                            dve.wait_ge(whole_ready, 2 * n + s + 1)
                            dve.tensor_tensor(by_cos[:, s], w["cos"], side_ps[:, s, 0], ALU.mult
                                              ).then_inc(turned_ready, 1)
                            dve.tensor_tensor(by_sin[:, s], w["sin"], side_ps[:, s, 1], ALU.mult
                                              ).then_inc(turned_ready, 1)
                    for s in range(2):
                        dve.wait_ge(cast, 4 * n + s + 1)
                        dve.wait_ge(low_ready, 2 * n + s + 1)
                        dve.tensor_tensor(rest[:, s, u], whole[:, s, u], parts[:, 0, s, u], ALU.subtract
                                          ).then_inc(rest_ready, 1)
                    dve.wait_ge(v_mm, 2 + n + 1)
                    dve.wait_ge(stored[u], 16 * STORES * (i + 1))
                    dve.tensor_tensor(v_sb[:, u].rearrange("p c d -> p (c d)"), w["bv"], v_ps[:, u], ALU.add
                                      ).then_inc(v_ready, 1)

        @block.gpsimd
        def _(pool):
            pool.sem_inc(low_ready, 4)
            if rotary:
                pool.sem_inc(whole_ready, 2)
            with pool.Fori(0, NB // 2) as i:
                for u in range(2):
                    n = 2 * i + u
                    if rotary:
                        for s in range(2):
                            pool.wait_ge(turned_ready, 4 * n + 2 * s + 2)
                            pool.wait_ge(rest_ready, 2 * n + s + 1)
                            pool.tensor_tensor(whole[:, s, u], by_cos[:, s], by_sin[:, s], ALU.add
                                               ).then_inc(whole_ready, 1)
                    pool.wait_ge(stored[u], 16 * STORES * (i + 1))
                    for s in range(2):
                        pool.wait_ge(cast, 4 * n + 2 + s + 1)
                        pool.tensor_tensor(parts[:, 2, s, u], rest[:, s, u], parts[:, 1, s, u], ALU.subtract
                                           ).then_inc(low_ready, 1)

        @block.sync
        def _(sp):
            for u in range(2):
                sp.sem_inc(stored[u], 16 * STORES)

            def store(n, u):
                for first, count in STEPS:
                    for s in range(2):
                        dst = stacks[s][ds(n, 1), :, first:first + count].rearrange("a p r t -> (a p) r t")
                        src = (parts[:, Q_PARTS[first], 0, u].unsqueeze(1).to_broadcast([P, count, T]) if s == 0
                               else parts[:, 0:count, 1, u])
                        sp.dma_start(dst, src).then_inc(stored[u], 16)
                dst = v_dram[ds(n, 1)].rearrange("a p c g d -> (a p) (c g d)")
                sp.dma_start(dst, v_sb[:, u].rearrange("p c d -> p (c d)")).then_inc(stored[u], 16)

            with sp.Fori(0, NB // 2) as i:
                for u in range(2):
                    n = 2 * i + u
                    sp.wait_ge(v_ready, 2 + n + 1)
                    sp.wait_ge(cast, 4 * n + 4)
                    sp.wait_ge(low_ready, 4 + 2 * n + 2)
                    store(n, u)
            store(NB, 1)
            sp.wait_ge(stored[0], 16 * STORES * (NB // 2 + 1))
            sp.wait_ge(stored[1], 16 * STORES * (NB // 2 + 2))


def attend(core, x, stacks, v_dram, shift_dram, w, scale, causal, bias=None):
    AHEAD = 3
    if causal:
        tiles = [[(0, 512, 0, 0)], [(0, 384, 1, 128)], [(0, 256, 2, 256), (256, 128, 3, 384)]]
    else:
        tiles = [[(0, T, k, 0)] for k in range(4)]
    if causal:
        order = [("T", 0), ("S", 0), ("T", 1), ("S", 1), ("S", 2), ("S", 3), ("T", 2), ("PV", 0)]
    else:
        order = [("T", 0), ("S", 0), ("T", 1), ("S", 1), ("T", 2), ("S", 2), ("PV", 0), ("T", 3), ("S", 3)]
    NTILE = len(tiles)
    tile_width = [sum(width for _, width, _, _ in tile) for tile in tiles]
    tile_at = [sum(tile_width[:i]) for i in range(NTILE)]
    place = {c: tile_at[i] + at for i, tile in enumerate(tiles) for at, _, c, _ in tile}
    T_BANKS, S_BANKS = 2, 4
    ADDED = (0, 1) if bias is not None else ()
    assert not ADDED or (NTILE == 3 and T_BANKS == 2)
    with core.phase() as ph:
        s_q, s_k = ph.sb("s_q", [P, 2, 4, T], BF16), ph.sb("s_k", [P, 2, 4, T], BF16)
        t_q, t_k = ph.sb("t_q", [P, 2, 4, T], BF16), ph.sb("t_k", [P, 2, 4, T], BF16)
        v_raw, v_st = ph.sb("v_raw", [P, 2, 4, 4, DK]), ph.sb("v_st", [P, 2, 4, 4, 32])
        ones = ph.sb("ones", [P, 4, 4, DK])
        probs = ph.sb("probs", [P, 2, 4, sum(tile_width)])
        row_max = ph.sb("row_max", [P, 2, 4, 4])
        shift = ph.sb("shift", [16, 2, SHIFT_ROWS, P], BF16)
        o_sb = ph.sb("o_sb", [P, T])
        inv = ph.sb("inv", [P, 4, 4])
        o_n = ph.sb("o_n", [P, 4, HEADS, DK])
        o_cat = ph.sb("o_cat", [P, T])
        t_ps, s_ps = ph.ps("t_ps", [P, T_BANKS, T]), ph.ps("s_ps", [P, S_BANKS, T])
        o_ps, misc = ph.ps("o_ps", [P, T]), ph.ps("misc", [P, T])
        zeroed = ph.sem("zeroed")
        s_loaded = [ph.sem(f"s_loaded{u}") for u in range(2)]
        t_loaded = [ph.sem(f"t_loaded{u}") for u in range(2)]
        v_loaded = [ph.sem(f"v_loaded{u}") for u in range(2)]
        m_stored = [ph.sem(f"m_stored{u}") for u in range(2)]
        s_mm = ph.sem("s_mm")
        s_read = ph.sem("s_read")
        t_mm = ph.sem("t_mm")
        expd = ph.sem("expd")
        pv_mm = ph.sem("pv_mm")
        v_ready = ph.sem("v_ready")
        evacuated = ph.sem("evacuated")
        biased = ph.sem("biased")
        misc_mm = ph.sem("misc_mm")
        misc_read = ph.sem("misc_read")
        shift_ready = ph.sem("shift_ready")
        divided = ph.sem("divided")
        block = ph.block()

        USES = [(0, "MT"), (0, "OT"), (1, "MT"), (1, "OT"), (1, "BT"), (2, "MT"), (2, "OT"), (2, "WO"),
                (3, "MT"), (3, "OT")]
        FIRST = [(0, "MT"), (1, "MT"), (2, "MT"), (2, "OT"), (3, "MT"), (3, "OT")]
        LEAD = 2

        def use_no(b, g, what):
            if isinstance(b, int) and b == 0:
                return LEAD + FIRST.index((g, what))
            return LEAD + len(FIRST) + len(USES) * (b - 1) + USES.index((g, what))

        def spread(b, k):
            return b + k // 4, k % 4

        @block.sync
        def _(sp):
            def load_s(b, k):
                bb, g = spread(b, k)
                for dst, src in ((s_q, stacks[0]), (s_k, stacks[1])):
                    sp.dma_start(dst[0:ROWS, g % 2],
                                 src[ds(bb, 1), 4 * DK * g:4 * DK * (g + 1)].rearrange("a (h d) r t -> (a d r) h t", h=4)
                                 ).then_inc(s_loaded[g % 2], 16)

            def load_t(b, k):
                bb, g = spread(b, k)
                for dst, src in ((t_q, stacks[0]), (t_k, stacks[1])):
                    sp.dma_start(dst[0:ROWS, g % 2],
                                 src[ds(bb, 1), 4 * DK * g:4 * DK * (g + 1)].rearrange("a (h d) r t -> (a d r) h t", h=4)
                                 ).then_inc(t_loaded[g % 2], 16)
                sp.wait_ge(m_stored[g % 2], 16 * (2 * bb + g // 2) + 16)
                sp.dma_start(t_q[ROWS:ROWS + SHIFT_ROWS, g % 2].rearrange("r h (c t) -> r (h c) t", c=4),
                             shift_dram[ds(bb, 1), 4 * g:4 * g + 4].rearrange("a h c r t -> (a r) (h c) t")
                             ).then_inc(t_loaded[g % 2], 16)
                sp.dma_start(v_raw[:, g % 2].rearrange("p c j d -> p c (j d)"),
                             v_dram[ds(bb, 1), :, :, g].rearrange("a p c d -> (a p) c d")
                             ).then_inc(v_loaded[g % 2], 16)

            def store_m(b, k):
                bb, g = spread(b, k)
                sp.wait_ge(shift_ready, 2 * (4 * bb + g) + 2)
                sp.dma_start(shift_dram[ds(bb, 1), 4 * g:4 * g + 4].rearrange("a h c r t -> (a h c) r t"),
                             shift[:, g % 2]).then_inc(m_stored[g % 2], 16)

            sp.wait_ge(zeroed, 5)
            load_s(0, 0)
            load_s(0, 1)
            for k in range(2, 4):
                sp.wait_ge(s_mm, 16 * (k - 2) + 16)
                load_s(0, k)
            store_m(0, 0)
            store_m(0, 1)
            load_t(0, 0)

            def step(b, g):
                n = 4 * b + g
                sp.wait_ge(s_mm, 16 * (n + 2) + 16)
                load_s(b, g + 4)
                if not (isinstance(b, int) and n == 0):
                    sp.wait_ge(t_mm, 4 * NTILE * n)
                sp.wait_ge(v_ready, n + 1 + 1)
                load_t(b, g + 1)
                store_m(b, g + 2)

            for g in range(4):
                step(0, g)
            with sp.Fori(1, NB) as b:
                for g in range(4):
                    step(b, g)
            sp.wait_ge(s_loaded[0], 32 * 34)
            sp.wait_ge(s_loaded[1], 32 * 34)
            sp.wait_ge(t_loaded[0], 48 * 33)
            sp.wait_ge(t_loaded[1], 48 * 32)
            sp.wait_ge(v_loaded[0], 16 * 33)
            sp.wait_ge(m_stored[0], 16 * 33)
            sp.wait_ge(m_stored[1], 16 * 33)

        @block.gpsimd
        def _(pool):
            pool.memset(s_q[:, :, :, :], 0.0).then_inc(zeroed, 1)
            pool.memset(s_k[:, :, :, :], 0.0).then_inc(zeroed, 1)
            pool.memset(t_q[:, :, :, :], 0.0).then_inc(zeroed, 1)
            pool.memset(t_k[:, :, :, :], 1.0).then_inc(zeroed, 1)
            pool.memset(v_st[:, :, :, :, :], 0.0).then_inc(zeroed, 1)
            pool.wait_ge(zeroed, 5)
            pool.memset(v_st[:, :, :, :, DK:DK + 1], 1.0).then_inc(zeroed, 1)
            pool.memset(ones[:, :, :, :], 1.0).then_inc(zeroed, 1)
            pool.wait_ge(zeroed, 7)
            pool.sem_inc(v_ready, 2)
            with pool.Fori(0, NB) as b:
                for g in range(4):
                    n = 4 * b + g
                    pool.wait_ge(v_loaded[g % 2], 16 * (2 * b + g // 2) + 16)
                    pool.wait_ge(pv_mm, n + 1)
                    pool.tensor_tensor(v_st[:, g % 2, :, :, 0:DK], v_raw[:, g % 2], ones[:, :, :, :], ALU.mult
                                       ).then_inc(v_ready, 1)

        @block.tensor
        def _(pe):
            pe.sem_inc(pv_mm, 2)
            pe.wait_ge(zeroed, 7)

            def scores_s(b, k, j, c):
                bb, g = spread(b, k)
                if j == 0 and c == 0:
                    pe.wait_ge(s_loaded[g % 2], 32 * (2 * bb + g // 2) + 32)
                no = ((4 * bb + g) * 4 + j) * 4 + c
                width = (c + 1) * P if causal else T
                out = s_ps[:, c % S_BANKS]
                pe.wait_ge(s_read, no + 1)
                mm = pe.matmul(out[:, 0:width], s_q[:, g % 2, j, c * P:(c + 1) * P], s_k[:, g % 2, j, 0:width],
                               start=True, stop=not causal)
                if bias is not None:
                    mm = pe.matmul(out[:, 0:width], bias["flip"], bias["s"][:, 4 * g + j, T - width:T],
                                   start=False, stop=True)
                elif causal:
                    mm = pe.matmul(out[:, width - P:width], w["ident16"], w["mask_s"], start=False, stop=True)
                mm.then_inc(s_mm, 1)

            def scores_t(b, g, j, i):
                no = ((4 * b + g) * 4 + j) * NTILE + i
                if j == 0 and i == 0:
                    pe.wait_ge(t_loaded[g % 2], 48 * (2 * b + g // 2) + 48)
                if ADDED and i != 1:
                    pe.wait_ge(biased, 2 + 2 * ((4 * b + g) * 4 + j) + i // 2)
                else:
                    pe.wait_ge(expd, no + 1)
                for at, width, c, first in tiles[i]:
                    out = t_ps[:, (j * NTILE + i) % T_BANKS, at:at + width]
                    mm = pe.matmul(out, t_k[:, g % 2, j, c * P:(c + 1) * P], t_q[:, g % 2, j, first:first + width],
                                   start=True, stop=i in ADDED or (bias is None and not (causal and first == c * P)))
                    if i in ADDED:
                        continue
                    if bias is not None:
                        for r in range(3):
                            mm = pe.matmul(out, bias["flip"],
                                           bias["t"][r][:, 4 * g + j, first - c * P:first - c * P + width],
                                           start=False, stop=(r == 2))
                    elif causal and first == c * P:
                        mm = pe.matmul(out[:, 0:P], w["ident16"], w["mask_t"], start=False, stop=True)
                mm.then_inc(t_mm, 1)

            def pv(b, k, c):
                n, g = 4 * b + k, k % 4
                if c == 0:
                    pe.wait_ge(expd, T_BANKS + 4 * NTILE * (n + 1))
                    pe.wait_ge(v_ready, 2 + n + 1)
                    pe.wait_ge(evacuated, n + 1)
                first = c * P if causal else 0
                for j in range(4):
                    mm = pe.matmul(o_ps[32 * j:32 * j + 32, first:T], v_st[:, g % 2, c, j, :],
                                   probs[:, g % 2, j, place[c]:place[c] + T - first], start=(c == 0), stop=(c == 3))
                if c == 3:
                    mm.then_inc(pv_mm, 1)

            def use(no):
                pe.wait_ge(misc_read, no)

            def mt(no, b, k):
                bb, g = spread(b, k)
                if not (isinstance(no, int) and no == 0):
                    use(no)
                pe.wait_ge(s_read, S_BANKS + 16 * (4 * bb + g) + 16)
                pe.transpose(misc[0:16, 0:P], row_max[:, g % 2].rearrange("p j c -> p (j c)"), w["ident"]
                             ).then_inc(misc_mm, 1)

            def ot(no, b, k):
                use(no)
                pe.wait_ge(evacuated, 1 + 4 * b + k + 1)
                for c in range(4):
                    mm = pe.transpose(misc[:, c * P:(c + 1) * P], o_sb[:, c * P:(c + 1) * P], w["ident"])
                mm.then_inc(misc_mm, 1)

            def bt(no, b):
                use(no)
                pe.wait_ge(divided, 2 * (4 * b + 3) + 2)
                for c in range(4):
                    mm = pe.transpose(misc[:, c * P:(c + 1) * P], o_n[:, c].rearrange("p h d -> p (h d)"), w["ident"])
                mm.then_inc(misc_mm, 1)

            def wo(no):
                use(no)
                pe.matmul(misc[:, :], w["wo"], o_cat[:, :], start=True, stop=True).then_inc(misc_mm, 1)

            for k in range(3):
                for j in range(4):
                    for c in range(4):
                        scores_s(0, k, j, c)
                if k:
                    mt(k - 1, 0, k - 1)

            def step(b, g):
                started = 4 * b + g if isinstance(b, int) else 99
                for j in range(4):
                    for what, i in order:
                        if what == "S":
                            scores_s(b, g + AHEAD, j, i)
                        elif what == "T":
                            scores_t(b, g, j, i)
                        elif started >= 1:
                            pv(b, g - 1, j) if g else pv(b - 1, 3, j)
                    if j == 0:
                        mt(use_no(b, g, "MT"), b, g + 2)
                    if j == 1 and started >= 2:
                        ot(use_no(b, g, "OT"), b, g - 2) if g >= 2 else ot(use_no(b, g, "OT"), b - 1, g + 2)
                    if j == 2 and g == 2 and started >= 4:
                        wo(use_no(b, g, "WO"))
                    if j == 3 and g == 1 and started >= 4:
                        bt(use_no(b, g, "BT"), b - 1)

            for g in range(4):
                step(0, g)
            with pe.Fori(1, NB) as b:
                for g in range(4):
                    step(b, g)
            last = use_no(NB, 0, "MT")
            for c in range(4):
                pv(NB - 1, 3, c)
            ot(last, NB - 1, 2)
            ot(last + 1, NB - 1, 3)
            bt(last + 2, NB - 1)
            wo(last + 3)

        @block.scalar
        def _(act):
            act.sem_inc(expd, T_BANKS)
            act.sem_inc(evacuated, 1)

            def evacuate(b, k, before):
                act.wait_ge(pv_mm, 2 + 4 * b + k + 1)
                if before is not None:
                    act.wait_ge(misc_mm, before + 1)
                act.activation(o_sb[:, :], o_ps[:, :], ACT.Copy).then_inc(evacuated, 1)

            def step(b, g):
                started = 4 * b + g if isinstance(b, int) else 99
                for j in range(4):
                    for i in range(NTILE):
                        act.wait_ge(t_mm, ((4 * b + g) * 4 + j) * NTILE + i + 1)
                        if j == 0 and i == 0:
                            act.wait_ge(pv_mm, 4 * b + g + 1)
                        exps = probs[:, g % 2, j, tile_at[i]:tile_at[i] + tile_width[i]]
                        tile = t_ps[:, (j * NTILE + i) % T_BANKS, 0:tile_width[i]]
                        if i in ADDED:
                            act.wait_ge(biased, 2 + 2 * ((4 * b + g) * 4 + j) + i + 1)
                            tile = exps
                        act.activation(exps, tile, ACT.Exp, scale=scale).then_inc(expd, 1)
                        if j == 0 and i == 0 and started >= 2:
                            before = None
                            if started >= 3:
                                before = use_no(b, g - 1, "OT") if g else use_no(b - 1, 3, "OT")
                            evacuate(b, g - 2, before) if g >= 2 else evacuate(b - 1, g + 2, before)

            for g in range(4):
                step(0, g)
            with act.Fori(1, NB) as b:
                for g in range(4):
                    step(b, g)
            last = use_no(NB, 0, "MT")
            evacuate(NB - 1, 2, use_no(NB - 1, 3, "OT"))
            evacuate(NB - 1, 3, last)

        @block.vector
        def _(dve):
            dve.sem_inc(s_read, S_BANKS)
            dve.sem_inc(biased, 2)

            def maxima(b, k, j, pieces=range(4)):
                bb, g = spread(b, k)
                for c in pieces:
                    width = (c + 1) * P if causal else T
                    dve.wait_ge(s_mm, ((4 * bb + g) * 4 + j) * 4 + c + 1)
                    dve.tensor_reduce(row_max[:, g % 2, j, c:c + 1], s_ps[:, c % S_BANKS, 0:width], X, ALU.max
                                      ).then_inc(s_read, 1)

            def add_bias(b, g, j, i):
                (_, width, c, first), = tiles[i]
                no = ((4 * b + g) * 4 + j) * NTILE + i
                dve.wait_ge(t_mm, no + 1)
                if j == 0 and i == 0:
                    dve.wait_ge(pv_mm, 4 * b + g + 1)
                dve.tensor_tensor(probs[:, g % 2, j, tile_at[i]:tile_at[i] + width],
                                  t_ps[:, (j * NTILE + i) % T_BANKS, 0:width],
                                  bias["t_whole"][:, 4 * g + j, first - c * P:first - c * P + width], ALU.add
                                  ).then_inc(biased, 1)

            def shifts(no, b, k):
                bb, g = spread(b, k)
                n = 4 * bb + g
                dve.wait_ge(misc_mm, no + 1)
                if not (isinstance(n, int) and n < 2):
                    dve.wait_ge(m_stored[g % 2], 16 * (2 * bb + g // 2))
                dve.tensor_scalar(shift[:, g % 2, 0], misc[0:16, 0:P], -1.0, None, ALU.mult).then_inc(shift_ready, 1)
                dve.wait_ge(shift_ready, 2 * n + 1)
                dve.scalar_tensor_tensor(shift[:, g % 2, 1], misc[0:16, 0:P], -1.0, shift[:, g % 2, 0],
                                         ALU.mult, ALU.subtract).then_inc(shift_ready, 1)
                dve.wait_ge(shift_ready, 2 * n + 2)
                dve.sem_inc(misc_read, 1)

            def divide(no, b, k):
                n, g = 4 * b + k, k % 4
                view = misc[:, :].rearrange("p (c j d) -> p c j d", c=4, j=4)
                dve.wait_ge(misc_mm, no + 1)
                dve.reciprocal(inv[:, :, :], view[:, :, :, DK]).then_inc(divided, 1)
                dve.wait_ge(divided, 2 * n + 1)
                dve.tensor_tensor(o_n[:, :, 4 * g:4 * g + 4, :], view[:, :, :, 0:DK],
                                  inv[:, :, :].unsqueeze(3).to_broadcast([P, 4, 4, DK]), ALU.mult
                                  ).then_inc(divided, 1)
                dve.wait_ge(divided, 2 * n + 2)
                dve.sem_inc(misc_read, 1)

            def gather(no):
                dve.wait_ge(misc_mm, no + 1)
                dve.tensor_copy(o_cat[:, :], misc[:, :]).then_inc(misc_read, 1)

            def add(no, b):
                dve.wait_ge(misc_mm, no + 1)
                dve.scalar_tensor_tensor(tok(x, b), misc[:, :], w["bo"], tok(x, b), ALU.add, ALU.add
                                         ).then_inc(misc_read, 1)

            for k in range(3):
                for j in range(4):
                    maxima(0, k, j)
                if k:
                    shifts(k - 1, 0, k - 1)

            def step(b, g):
                started = 4 * b + g if isinstance(b, int) else 99
                for j in range(4):
                    if ADDED:
                        add_bias(b, g, j, 0)
                    maxima(b, g + AHEAD, j, (0, 1) if ADDED else range(4))
                    if ADDED:
                        add_bias(b, g, j, 1)
                        maxima(b, g + AHEAD, j, (2, 3))
                    if j == 0:
                        shifts(use_no(b, g, "MT"), b, g + 2)
                    if j == 1 and started >= 2:
                        divide(use_no(b, g, "OT"), b, g - 2) if g >= 2 else divide(use_no(b, g, "OT"), b - 1, g + 2)
                    if j == 2 and g == 2 and started >= 4:
                        add(use_no(b, g, "WO"), b - 1)
                    if j == 3 and g == 1 and started >= 4:
                        gather(use_no(b, g, "BT"))

            for g in range(4):
                step(0, g)
            with dve.Fori(1, NB) as b:
                for g in range(4):
                    step(b, g)
            last = use_no(NB, 0, "MT")
            divide(last, NB - 1, 2)
            divide(last + 1, NB - 1, 3)
            gather(last + 2)
            add(last + 3, NB - 1)


STATE, RANK, TAPS = 16, 8, 4
BC = 2 * STATE
KINDS = 6


REL = T + P


def relative_bias(core, rel, rel_back, rel_dram, whole_dram, t_bias, t_whole, s_bias, flip16):
    with core.phase() as ph:
        raw, rest = ph.sb("raw", [HEADS, 2, REL]), ph.sb("rest", [HEADS, REL])
        part = ph.sb("part", [HEADS, 4, REL], BF16)
        back = ph.sb("back", [P, HEADS, T])
        flip = ph.sb("flip", [P, P])
        turned_ps = ph.ps("turned_ps", [P, 4, T])
        back_loaded = [ph.sem(f"back_loaded{g}") for g in range(4)]
        turned = ph.sem("turned")
        copied = ph.sem("copied")
        flip_ready = ph.sem("flip_ready")
        loaded, made, stored, windows = ph.sem("loaded"), ph.sem("made"), ph.sem("stored"), ph.sem("windows")
        block = ph.block()

        @block.sync
        def _(sp):
            sp.dma_start(raw[:, 0], rel).then_inc(loaded, 16)
            sp.dma_start(raw[:, 1], rel_back).then_inc(loaded, 16)
            sp.wait_ge(made, 9)
            sp.dma_start(rel_dram.ap().rearrange("r h i -> h r i"), part[:, :, :]).then_inc(stored, 16)
            sp.dma_start(whole_dram.ap(), raw[:, 0]).then_inc(stored, 16)
            sp.wait_ge(stored, 32)
            for g in range(4):
                src = bass.AP(tensor=whole_dram, offset=4 * g * REL, ap=[[1, P], [REL, 4], [1, T]])
                sp.dma_start(back[:, 4 * g:4 * g + 4], src).then_inc(back_loaded[g], 16)
            for r, dst in enumerate(t_bias + [s_bias[:, :, :]]):
                src = bass.AP(tensor=rel_dram, offset=r * HEADS * REL, ap=[[1, P], [REL, HEADS], [1, dst.shape[-1]]])
                sp.dma_start(dst, src).then_inc(windows, 16)
            sp.wait_ge(windows, 16 * 4)

        @block.tensor
        def _(pe):
            pe.wait_ge(flip_ready, 1)
            for head in range(HEADS):
                if head % 4 == 0:
                    pe.wait_ge(back_loaded[head // 4], 16)
                pe.wait_ge(copied, head + 1)
                pe.matmul(turned_ps[:, head % 4], flip[:, :], back[:, head], start=True, stop=True
                          ).then_inc(turned, 1)

        @block.scalar
        def _(act):
            act.sem_inc(copied, 4)
            for head in range(HEADS):
                act.wait_ge(turned, head + 1)
                act.activation(t_whole[:, head], turned_ps[:, head % 4], ACT.Copy).then_inc(copied, 1)

        @block.vector
        def _(dve):
            made_no = [0]

            def made_next(ins):
                made_no[0] += 1
                ins.then_inc(made, 1)
                dve.wait_ge(made, made_no[0])

            dve.tensor_copy(flip[:, :], flip16).then_inc(flip_ready, 1)
            dve.wait_ge(loaded, 32)
            made_next(dve.tensor_scalar(raw[:, :, :], raw[:, :, :], float(DK ** 0.5), None, ALU.mult))
            made_next(dve.memset(raw[:, 0, 0:P - 1], MASKED))
            made_next(dve.memset(raw[:, 1, T:REL - 1], MASKED))
            made_next(dve.tensor_copy(part[:, 0], raw[:, 0]))
            made_next(dve.tensor_tensor(rest[:, :], raw[:, 0], part[:, 0], ALU.subtract))
            made_next(dve.tensor_copy(part[:, 1], rest[:, :]))
            made_next(dve.tensor_tensor(rest[:, :], rest[:, :], part[:, 1], ALU.subtract))
            made_next(dve.tensor_copy(part[:, 2], rest[:, :]))
            made_next(dve.tensor_copy(part[:, 3], raw[:, 1]))


def mamba_in(core, xn, mamba_dram, bc_dram, w):
    with core.phase() as ph:
        late = ph.sb("late", [P, 2, TAPS - 1 + T])
        conv = ph.sb("conv", [P, 2, 2, T])
        out = ph.sb("out", [P, 2, KINDS, T])
        dbl = ph.sb("dbl", [BC + RANK, T])
        high, middle = ph.sb("high", [BC, 2, T], BF16), ph.sb("middle", [BC, 2, T], BF16)
        low, rest = ph.sb("low", [BC, 2, T], BF16), ph.sb("rest", [BC, T])
        in_ps, dbl_ps, dt_ps = ph.ps("in_ps", [P, 4, T]), ph.ps("dbl_ps", [P, T]), ph.ps("dt_ps", [P, 2, T])
        padded = ph.sem("padded")
        in_mm = ph.sem("in_mm")
        taken = ph.sem("taken")
        tapped = ph.sem("tapped")
        xc_ready = ph.sem("xc_ready")
        dbl_mm = ph.sem("dbl_mm")
        dbl_ready = ph.sem("dbl_ready")
        cast = ph.sem("cast")
        low_ready = ph.sem("low_ready")
        dt_mm = ph.sem("dt_mm")
        dt_ready = ph.sem("dt_ready")
        stored = [ph.sem(f"stored{u}") for u in range(2)]
        STORES = 4
        block = ph.block()

        @block.tensor
        def _(pe):
            pe.sem_inc(dt_mm, 2)

            def inward(n):
                if not (isinstance(n, int) and n == 0):
                    pe.wait_ge(taken, 6 * n)
                for h in range(4):
                    pe.matmul(in_ps[:, h], w["in_w"][:, h], tok(xn, n), start=True, stop=True).then_inc(in_mm, 1)

            def onward(n, u):
                pe.wait_ge(xc_ready, 2 + 2 * n + 2)
                if not (isinstance(n, int) and n == 0):
                    pe.wait_ge(dbl_ready, 2 * n)
                for h in range(2):
                    mm = pe.matmul(dbl_ps[0:BC + RANK, :], w["x_w"][:, h], out[:, u, h],
                                   start=(h == 0), stop=(h == 1))
                mm.then_inc(dbl_mm, 1)
                pe.wait_ge(dbl_ready, 2 * n + 1)
                for h in range(2):
                    pe.wait_ge(dt_ready, 2 * n + h + 1)
                    pe.matmul(dt_ps[:, h], w["dt_w"][BC:BC + RANK, h], dbl[BC:BC + RANK, :], start=True, stop=True
                              ).then_inc(dt_mm, 1)

            inward(0)
            with pe.Fori(0, NB // 2 - 1) as i:
                for u in range(2):
                    inward(2 * i + u + 1)
                    onward(2 * i + u, u)
            inward(NB - 1)
            onward(NB - 2, 0)
            onward(NB - 1, 1)

        @block.scalar
        def _(act):
            act.sem_inc(xc_ready, 2)
            act.wait_ge(padded, 1)

            def step(n, u, t, first=False):
                act.wait_ge(tapped, 6 + 6 * n)
                act.wait_ge(xc_ready, 2 * n + 2)
                for h in range(2):
                    act.wait_ge(in_mm, 4 * n + h + 1)
                    act.activation(late[:, h, TAPS - 1:], in_ps[:, h], ACT.Copy).then_inc(taken, 1)
                    act.activation(conv[:, h, 0], in_ps[:, h], ACT.Identity, bias=w["conv_b"][:, h:h + 1],
                                   scale=w["conv_w"][:, h, TAPS - 1:TAPS]).then_inc(taken, 1)
                if not first:
                    cast_high(n - 1, 1 - u)
                act.wait_ge(stored[u], 16 * STORES * (t + 1))
                for h in range(2):
                    act.wait_ge(in_mm, 4 * n + 2 + h + 1)
                    act.activation(out[:, u, 2 + h], in_ps[:, 2 + h], ACT.Silu).then_inc(taken, 1)
                for h in range(2):
                    act.wait_ge(tapped, 6 + 6 * n + 3 * h + 3)
                    act.activation(out[:, u, h], conv[:, h, 1], ACT.Silu).then_inc(xc_ready, 1)
                if not first:
                    cast_middle(n - 1, 1 - u)

            def cast_high(n, u):
                act.wait_ge(dbl_ready, 2 * n + 1)
                act.activation(high[:, u], dbl_ps[0:BC, :], ACT.Copy).then_inc(cast, 1)

            def cast_middle(n, u):
                act.wait_ge(dbl_ready, 2 * n + 2)
                act.activation(middle[:, u], rest[:, :], ACT.Copy).then_inc(cast, 1)

            step(0, 0, 0, first=True)
            step(1, 1, 0)
            with act.Fori(1, NB // 2) as i:
                for u in range(2):
                    step(2 * i + u, u, i)
            cast_high(NB - 1, 1)
            cast_middle(NB - 1, 1)

        @block.vector
        def _(dve):
            dve.sem_inc(tapped, 6)
            dve.sem_inc(dt_ready, 2)
            dve.memset(late[:, :, 0:TAPS - 1], 0.0).then_inc(padded, 1)

            def taps(n):
                for h in range(2):
                    dve.wait_ge(taken, 6 * n + 2 * h + 2)
                    dve.wait_ge(xc_ready, 2 * n + h + 1)
                    for k in range(TAPS - 1):
                        if k:
                            dve.wait_ge(tapped, 6 + 6 * n + 3 * h + k)
                        dve.scalar_tensor_tensor(conv[:, h, (k + 1) % 2], late[:, h, k:k + T],
                                                 w["conv_w"][:, h, k:k + 1], conv[:, h, k % 2],
                                                 ALU.mult, ALU.add).then_inc(tapped, 1)

            def copy_dbl(n):
                dve.wait_ge(dbl_mm, n + 1)
                dve.wait_ge(dt_mm, 2 * n + 2)
                dve.tensor_copy(dbl[:, :], dbl_ps[0:BC + RANK, :]).then_inc(dbl_ready, 1)

            def split(n, u, t):
                dve.wait_ge(cast, 2 * n + 1)
                dve.wait_ge(low_ready, n + 1)
                dve.tensor_tensor(rest[:, :], dbl_ps[0:BC, :], high[:, u], ALU.subtract).then_inc(dbl_ready, 1)
                dve.wait_ge(stored[u], 16 * STORES * (t + 1))
                for h in range(2):
                    dve.wait_ge(dt_mm, 2 + 2 * n + h + 1)
                    dve.tensor_scalar(out[:, u, 4 + h], dt_ps[:, h], w["dt_b"][:, h:h + 1], None, ALU.add
                                      ).then_inc(dt_ready, 1)

            def step(n, u, t_before):
                copy_dbl(n - 1)
                taps(n)
                split(n - 1, 1 - u, t_before)

            taps(0)
            step(1, 1, 0)
            with dve.Fori(1, NB // 2) as i:
                for u in range(2):
                    step(2 * i + u, u, i - 1 + u)
            copy_dbl(NB - 1)
            split(NB - 1, 1, NB // 2 - 1)

        @block.gpsimd
        def _(pool):
            pool.sem_inc(low_ready, 1)
            with pool.Fori(0, NB // 2) as i:
                for u in range(2):
                    n = 2 * i + u
                    pool.wait_ge(stored[u], 16 * STORES * (i + 1))
                    pool.wait_ge(cast, 2 * n + 2)
                    pool.tensor_tensor(low[:, u], rest[:, :], middle[:, u], ALU.subtract).then_inc(low_ready, 1)

        @block.sync
        def _(sp):
            for u in range(2):
                sp.sem_inc(stored[u], 16 * STORES)

            def store(n, u):
                sp.dma_start(mamba_dram[ds(n, 1)].rearrange("a k p t -> (a p) k t"), out[:, u]
                             ).then_inc(stored[u], 16)
                for r, part in enumerate((high, middle, low)):
                    sp.dma_start(bc_dram[ds(n, 1), r].rearrange("a c t -> (a c) t"), part[:, u]
                                 ).then_inc(stored[u], 16)

            with sp.Fori(0, NB // 2) as i:
                for u in range(2):
                    n = 2 * i + u
                    sp.wait_ge(low_ready, 1 + n + 1)
                    sp.wait_ge(dt_ready, 2 + 2 * n + 2)
                    store(n, u)
            store(NB, 1)
            sp.wait_ge(stored[0], 16 * STORES * (NB // 2 + 1))
            sp.wait_ge(stored[1], 16 * STORES * (NB // 2 + 2))


def mamba_scan(core, x, mamba_dram, bc_dram, w):
    R = 8
    RS = 4
    RB = 4
    AHEAD = 3
    AT = 5
    with core.phase() as ph:
        inp = ph.sb("inp", [P, 2, KINDS, T])
        bc = ph.sb("bc", [3 * BC, 2, T], BF16)
        rate = ph.sb("rate", [P, 2, STATE])
        small = ph.sb("small", [P, 2, T])
        log1 = ph.sb("log1", [P, 2, T])
        lost = ph.sb("lost", [P, 2, T])
        dt, dtx = ph.sb("dt", [P, 2, 2, T]), ph.sb("dtx", [P, 2, 2, T])
        b_sb = ph.sb("b_sb", [P, RB, T])
        skip_w = ph.sb("skip_w", [P, 2, P])
        da, dbx = ph.sb("da", [P, R, T]), ph.sb("dbx", [P, R, T])
        state, prod = ph.sb("state", [P, RS, T]), ph.sb("prod", [P, RS, T])
        gated = ph.sb("gated", [P, 2, T])
        b_ps, c_ps = ph.ps("b_ps", [P, 2, T]), ph.ps("c_ps", [P, 2, T])
        y_ps, out_ps = ph.ps("y_ps", [P, 2, T]), ph.ps("out_ps", [P, T])
        loaded = [ph.sem(f"loaded{u}") for u in range(2)]
        select_loaded = ph.sem("select_loaded")
        rate_ready = ph.sem("rate_ready")
        soft = ph.sem("soft")
        back = ph.sem("back")
        mended = ph.sem("mended")
        dt_ready = ph.sem("dt_ready")
        dtx_ready = ph.sem("dtx_ready")
        b_mm = ph.sem("b_mm")
        b_ready = ph.sem("b_ready")
        c_mm = ph.sem("c_mm")
        da_ready = ph.sem("da_ready")
        dbx_ready = ph.sem("dbx_ready")
        scanned = ph.sem("scanned")
        prod_ready = ph.sem("prod_ready")
        acc_mm = ph.sem("acc_mm")
        skip_ready = ph.sem("skip_ready")
        gated_ready = ph.sem("gated_ready")
        out_mm = ph.sem("out_mm")
        added = ph.sem("added")
        block = ph.block()

        def k_slot(n, h, ring=R):
            return (2 * n + h) % ring

        @block.sync
        def _(sp):
            def load(b, u):
                sp.dma_start(inp[:, u], mamba_dram[ds(b, 1)].rearrange("a k p t -> (a p) k t")
                             ).then_inc(loaded[u], 16)
                sp.dma_start(bc[:, u], bc_dram[ds(b, 1)].rearrange("a r c t -> (a r c) t")).then_inc(loaded[u], 16)

            load(0, 0)
            sp.dma_start(w["select"], w["select_dram"]).then_inc(select_loaded, 16)
            load(1, 1)
            with sp.Fori(1, NB // 2) as i:
                for u in range(2):
                    b = 2 * i + u
                    sp.wait_ge(gated_ready, 2 * b)
                    load(b, u)
            sp.wait_ge(gated_ready, 2 * NB)
            load(NB, 0)
            sp.wait_ge(loaded[0], 32 * (NB // 2 + 1))
            sp.wait_ge(loaded[1], 32 * (NB // 2))

        @block.tensor
        def _(pe):
            pe.sem_inc(acc_mm, RS)
            pe.sem_inc(out_mm, 1)

            def inputs_loaded(b, u):
                pe.wait_ge(loaded[u], 32 * (b // 2) + 32 if isinstance(b, int) else 16 * (b - u) + 32)

            def broadcast_b(b, u, n):
                if n == 0:
                    inputs_loaded(b, u)
                pe.wait_ge(b_ready, STATE * b + n + 1)
                pe.matmul(b_ps[:, n % 2], w["select"][:, n], bc[:, u], start=True, stop=True).then_inc(b_mm, 1)

            def broadcast_c(b, u, n):
                if n == 0:
                    inputs_loaded(b, u)
                pe.wait_ge(prod_ready, RS - 4 + 2 * (STATE * b + n) + 2)
                pe.matmul(c_ps[:, n % 2], w["select"][:, STATE + n], bc[:, u], start=True, stop=True
                          ).then_inc(c_mm, 1)

            def outward(b):
                pe.wait_ge(gated_ready, 2 + 2 * b + 2)
                pe.wait_ge(added, b + 1)
                for h in range(2):
                    mm = pe.matmul(out_ps[:, :], w["out_w"][:, h], gated[:, h], start=(h == 0), stop=(h == 1))
                mm.then_inc(out_mm, 1)

            def sequence(b, u, first=False, last=False):
                for n in range(STATE):
                    if n + AHEAD < STATE:
                        broadcast_b(b, u, n + AHEAD)
                    elif not last:
                        broadcast_b(b + 1, 1 - u, n + AHEAD - STATE)
                    if n + 1 < STATE:
                        broadcast_c(b, u, n + 1)
                    elif not last:
                        broadcast_c(b + 1, 1 - u, 0)
                    for h in range(2):
                        k = 2 * (STATE * b + n) + h
                        if n == 0:
                            if not first:
                                pe.wait_ge(gated_ready, 2 * b + h + 1)
                            pe.matmul(y_ps[:, h], skip_w[:, h], inp[:, u, h], start=True, stop=False)
                        pe.wait_ge(prod_ready, RS + k + 1)
                        pe.matmul(y_ps[:, h], w["ident"], prod[:, k_slot(n, h, RS)], start=False,
                                  stop=(n == STATE - 1)).then_inc(acc_mm, 1)
                    if n == 4 and not first:
                        outward(b - 1)

            pe.wait_ge(select_loaded, 16)
            for n in range(AHEAD):
                broadcast_b(0, 0, n)
            broadcast_c(0, 0, 0)
            pe.wait_ge(skip_ready, 2)
            sequence(0, 0, first=True)
            sequence(1, 1)
            with pe.Fori(1, NB // 2 - 1) as i:
                for u in range(2):
                    sequence(2 * i + u, u)
            sequence(NB - 2, 0)
            sequence(NB - 1, 1, last=True)
            outward(NB - 1)

        @block.scalar
        def _(act):
            act.preload_act_table_set("natural_log_exp_and_others")
            act.sem_inc(b_ready, 2)

            def copy_b(b, n):
                m = STATE * b + n
                act.wait_ge(b_mm, m + 1)
                act.wait_ge(dbx_ready, R - 2 * RB + 2 * m + 2)
                act.activation(b_sb[:, n % RB], b_ps[:, n % 2], ACT.Copy).then_inc(b_ready, 1)

            act.activation(rate[:, :, :], w["a_log"], ACT.Exp).then_inc(soft, 1)

            def soften(b, u):
                act.wait_ge(loaded[u], 32 * (b // 2) + 32 if isinstance(b, int) else 16 * (b - u) + 32)
                for h in range(2):
                    base = 1 + 6 * b + 3 * h
                    act.wait_ge(dt_ready, 2 * b + h + 1)
                    act.activation(small[:, h], inp[:, u, 4 + h], ACT.Abs).then_inc(soft, 1)
                    act.wait_ge(soft, base + 1)
                    act.activation(small[:, h], small[:, h], ACT.Exp, scale=-1.0).then_inc(soft, 1)
                    act.wait_ge(soft, base + 2)
                    act.activation(log1[:, h], small[:, h], ACT.Ln, bias=w["one"]).then_inc(soft, 1)

            def sequence(b, u, last=False):
                for n in range(STATE):
                    m = STATE * b + n
                    copy_b(b, n)
                    for h in range(2):
                        k = 2 * m + h
                        if n == 0:
                            act.wait_ge(dt_ready, 2 + 2 * b + h + 1)
                        act.wait_ge(scanned, k + 1)
                        act.activation(da[:, k_slot(n, h)], dt[:, u, h], ACT.Exp, scale=rate[:, h, n:n + 1]
                                       ).then_inc(da_ready, 1)
                    if n == AT and not last:
                        soften(b + 1, 1 - u)

            act.wait_ge(rate_ready, 1)
            soften(0, 0)
            with act.Fori(0, NB // 2 - 1) as i:
                for u in range(2):
                    sequence(2 * i + u, u)
            sequence(NB - 2, 0)
            sequence(NB - 1, 1, last=True)

        @block.gpsimd
        def _(pool):
            pool.sem_inc(dbx_ready, R)

            def scale_input(b, u):
                for h in range(2):
                    pool.wait_ge(dt_ready, 2 + 2 * b + h + 1)
                    pool.tensor_tensor(dtx[:, u, h], dt[:, u, h], inp[:, u, h], ALU.mult).then_inc(dtx_ready, 1)

            def sequence(b, u, last=False):
                for n in range(STATE):
                    m = STATE * b + n
                    for h in range(2):
                        k = 2 * m + h
                        pool.wait_ge(b_ready, 2 + m + 1)
                        if n == 0:
                            pool.wait_ge(dtx_ready, 2 * b + h + 1)
                        pool.wait_ge(scanned, k + 1)
                        pool.tensor_tensor(dbx[:, k_slot(n, h)], dtx[:, u, h], b_sb[:, n % RB], ALU.mult
                                           ).then_inc(dbx_ready, 1)
                    if n == AT + 6 and not last:
                        scale_input(b + 1, 1 - u)

            scale_input(0, 0)
            sequence(0, 0)
            sequence(1, 1)
            with pool.Fori(1, NB // 2 - 1) as i:
                for u in range(2):
                    sequence(2 * i + u, u)
            sequence(NB - 2, 0)
            sequence(NB - 1, 1, last=True)

        @block.vector
        def _(dve):
            dve.sem_inc(scanned, R)
            dve.sem_inc(prod_ready, RS)
            dve.sem_inc(gated_ready, 2)
            dve.sem_inc(added, 1)
            dve.sem_inc(dt_ready, 2)
            dve.wait_ge(soft, 1)
            dve.tensor_scalar(rate[:, :, :], rate[:, :, :], -1.0, None, ALU.mult).then_inc(rate_ready, 1)
            for h in range(2):
                dve.tensor_scalar(skip_w[:, h], w["ident"], w["d"][:, h:h + 1], None, ALU.mult).then_inc(skip_ready, 1)

            def round_trip(b):
                for h in range(2):
                    dve.wait_ge(soft, 1 + 6 * b + 3 * h + 2)
                    dve.wait_ge(dt_ready, 2 * b + h + 1)
                    dve.tensor_scalar(lost[:, h], small[:, h], 1.0, -1.0, ALU.add, ALU.add).then_inc(back, 1)

            def mend(b):
                for h in range(2):
                    dve.wait_ge(back, 2 * b + h + 1)
                    dve.tensor_tensor(lost[:, h], small[:, h], lost[:, h], ALU.subtract).then_inc(mended, 1)
                for h in range(2):
                    dve.wait_ge(soft, 1 + 6 * b + 3 * h + 3)
                    dve.wait_ge(mended, 4 * b + h + 1)
                    dve.tensor_tensor(log1[:, h], log1[:, h], lost[:, h], ALU.add).then_inc(mended, 1)

            def step_size(b, u):
                for h in range(2):
                    dve.wait_ge(mended, 4 * b + 2 + h + 1)
                    dve.scalar_tensor_tensor(dt[:, u, h], inp[:, u, 4 + h], 0.0, log1[:, h], ALU.max, ALU.add
                                             ).then_inc(dt_ready, 1)

            def scan(b, n, h):
                k = 2 * (STATE * b + n) + h
                s, out = k_slot(n, h), k_slot(n, h, RS)
                dve.wait_ge(da_ready, k + 1)
                dve.wait_ge(dbx_ready, R + k + 1)
                dve.wait_ge(prod_ready, k + 1)
                dve.tensor_tensor_scan(out=state[:, out], data0=da[:, s], data1=dbx[:, s], initial=0.0,
                                       op0=ALU.mult, op1=ALU.add).then_inc(scanned, 1)

            def times_c(b, n, h):
                k = 2 * (STATE * b + n) + h
                s = k_slot(n, h, RS)
                dve.wait_ge(scanned, R + k + 1)
                dve.wait_ge(c_mm, STATE * b + n + 1)
                dve.wait_ge(acc_mm, k + 1)
                dve.tensor_tensor(prod[:, s], state[:, s], c_ps[:, n % 2], ALU.mult).then_inc(prod_ready, 1)

            def gate(b, u):
                for h in range(2):
                    dve.wait_ge(acc_mm, RS + 2 * STATE * b + 2 * STATE - 1 + h)
                    dve.wait_ge(out_mm, b + 1)
                    dve.tensor_tensor(gated[:, h], y_ps[:, h], inp[:, u, 2 + h], ALU.mult).then_inc(gated_ready, 1)

            def add(b):
                dve.wait_ge(out_mm, 1 + b + 1)
                dve.tensor_tensor(tok(x, b), tok(x, b), out_ps[:, :], ALU.add).then_inc(added, 1)

            def sequence(b, u, first=False, last=False):
                for n in range(STATE):
                    scan(b, n, 0)
                    scan(b, n, 1)
                    if n == 1 and not first:
                        gate(b - 1, 1 - u)
                    times_c(b, n, 0)
                    times_c(b, n, 1)
                    if n == 6 and not first:
                        add(b - 1)
                    if n == AT + 1 and not last:
                        round_trip(b + 1)
                    if n == AT + 2 and not last:
                        mend(b + 1)
                    if n == AT + 4 and not last:
                        step_size(b + 1, 1 - u)

            round_trip(0)
            mend(0)
            step_size(0, 0)
            sequence(0, 0, first=True)
            sequence(1, 1)
            with dve.Fori(1, NB // 2 - 1) as i:
                for u in range(2):
                    sequence(2 * i + u, u)
            sequence(NB - 2, 0)
            sequence(NB - 1, 1, last=True)
            gate(NB - 1, 1)
            add(NB - 1)


PHASES = ("norm", "attn_a0", "norm", "ffn0", "norm", "mamba", "norm", "ffn0", "norm", "attn_a1", "norm", "ffn1",
          "norm", "attn_b1", "norm", "ffn1")


SMALL16 = ("ident16", "mask_s", "mask_t", "flip")
SMALL = ("mean_mat", "eps", "ffn_w", "ffn_bias", "router", "earlier", "l0_w", "l0_b", "mla_w", "mla_b", "rot_w",
         "latent_w", "latent_b", "latent_kv", "in_w", "conv_w", "conv_b", "x_w", "dt_w", "dt_b", "a_log", "d", "out_w", "one") + SMALL16


def program(nc, a, out, phases=PHASES):
    with ExitStack() as ctx:
        core = Core(nc, ctx)

        def sb(name, shape, dt=F32):
            return ctx.enter_context(nc.sbuf_tensor(name, shape, dt))

        x, xn = sb("x", [P, NTOK]), sb("xn", [P, NTOK])
        small = {}
        loads = []
        for name in SMALL:
            small[name] = sb("c_" + name, list(a[name].shape), BF16 if name in SMALL16 else F32)
            loads.append((small[name].ap(), a[name]))
        ident = sb("c_ident", [P, P])
        load_x(core, a["x"], x, (ident, a["ident"]), loads)
        stacks = [nc.dram_tensor(f"stack_{s}", [NB + 1, P, PLACES, T], BF16).ap() for s in "qk"]
        shift_dram = nc.dram_tensor("shifts", [NB + 1, HEADS, 4, SHIFT_ROWS, P], BF16).ap()
        v_dram = nc.dram_tensor("values", [NB + 1, P, 4, 4, 32], F32).ap()
        masks = {name: small[name][:, :] for name in ("ident16", "mask_s", "mask_t")}
        rel_dram = nc.dram_tensor("relative_bias_parts", [4, HEADS, REL], BF16)
        whole_dram = nc.dram_tensor("relative_bias", [HEADS, REL], F32)
        mamba_dram = nc.dram_tensor("mamba_inputs", [NB + 1, KINDS, P, T], F32).ap()
        bc_dram = nc.dram_tensor("mamba_bc", [NB + 1, 3, BC, T], BF16).ap()
        masks["ident"] = ident[:, :]
        route_dram = nc.dram_tensor("route_weights", [4, P, P], F32).ap()
        for name in phases:
            if name == "norm":
                layer_norm(core, x, xn, small["mean_mat"], small["eps"])
            elif name == "ffn0":
                recurrent_ffn(core, x, xn, small["ffn_w"], small["ffn_bias"])
            elif name == "ffn1":
                experts(core, x, xn, a["w1"], a["w2"], route_dram, small["router"], small["earlier"], ident)
            elif name == "mamba":
                mw = {k: small[k] for k in ("in_w", "conv_w", "conv_b", "x_w", "dt_w", "dt_b", "out_w", "d")}
                mamba_in(core, xn, mamba_dram, bc_dram, mw)
                mw.update(a_log=small["a_log"][:, :, :], ident=ident[:, :], one=small["one"][:, 0:1])
                select = xn[0:3 * BC, :].bitcast(BF16)[:, 0:2 * STATE * P].rearrange("p (s c) -> p s c", c=P)
                mw.update(select=select, select_dram=a["select"])
                mamba_scan(core, x, mamba_dram, bc_dram, mw)
            elif name == "attn_a0":
                lb = small["l0_b"]
                with core.phase() as ph:
                    bv = ph.sb("bv", [P, 4 * P])
                    load_once(core, [(bv[:, :], a["l0_bv"])])
                    lw = small["l0_w"]
                    project(core, xn, stacks, v_dram, dict(wq=lw[:, 0], wk=lw[:, 1], wv=lw[:, 2],
                                                           bq=lb[:, 0:1], bk=lb[:, 1:2], bv=bv[:, :]))
                with core.phase() as ph:
                    parts = ph.sb("bias_parts", [P, 3, HEADS, T // 2], BF16)
                    s_bias = ph.sb("s_bias", [P, HEADS, T], BF16)
                    t_whole = xn[:, :].rearrange("p (h t) -> p h t", h=HEADS)
                    t_bias = [parts[:, j] for j in range(3)]
                    relative_bias(core, a["rel"], a["rel_back"], rel_dram, whole_dram, t_bias, t_whole, s_bias,
                                  small["flip"][:, :])
                    attend(core, x, stacks, v_dram, shift_dram, dict(masks, wo=small["l0_w"][:, 3], bo=lb[:, 2:3]),
                           DK ** -0.5, causal=True,
                           bias=dict(flip=small["flip"][:, :], t=t_bias, t_whole=t_whole, s=s_bias))
            elif name == "attn_a1":
                lw, mb = small["latent_w"], small["mla_b"]
                with core.phase() as ph:
                    bv = ph.sb("bv", [P, 4 * P])
                    load_once(core, [(bv[:, :], a["mla_bv"])])
                    project(core, xn, stacks, v_dram, dict(
                        wq=small["mla_w"][:, 0], wl=lw[:, :], bl=small["latent_b"][0:32, 0:1],
                        wk=small["latent_kv"][:, 0], wv=small["latent_kv"][:, 1],
                        bq=mb[:, 0:1], bk=mb[:, 1:2], bv=bv[:, :]))
                attend(core, x, stacks, v_dram, shift_dram, dict(masks, wo=small["mla_w"][:, 1], bo=mb[:, 2:3]),
                       DK ** -0.5, causal=False)
            elif name == "attn_b1":
                with core.phase() as ph:
                    bv, cos, sin = ph.sb("bv", [P, 4 * P]), ph.sb("cos", [P, T]), ph.sb("sin", [P, T])
                    turned = ph.sb("turned", [P, 2, P])
                    load_once(core, [(cos[:, :], a["cos"]), (sin[:, :], a["sin"])], zero=bv, turn=(turned, small["rot_w"]))
                    project(core, xn, stacks, v_dram, dict(
                        wq=small["rot_w"][:, 0], wk=small["rot_w"][:, 1], wv=small["rot_w"][:, 2],
                        wq_turned=turned[:, 0], wk_turned=turned[:, 1], cos=cos[:, :], sin=sin[:, :], bv=bv[:, :]))
                attend(core, x, stacks, v_dram, shift_dram, dict(masks, wo=small["rot_w"][:, 3], bo=0.0),
                       DK ** -0.5, causal=True)
        store_x(core, out, x, ident)


def load_once(core, loads, zero=None, turn=None):
    with core.phase() as ph:
        loaded, made = ph.sem("loaded"), ph.sem("made")
        block = ph.block()

        @block.sync
        def _(sp):
            for dst, src in loads:
                sp.dma_start(dst, src).then_inc(loaded, 16)
            sp.wait_ge(loaded, 16 * len(loads))

        @block.vector
        def _(dve):
            if zero is not None:
                dve.memset(zero[:, :], 0.0).then_inc(made, 1)
            if turn is not None:
                dst, src = turn
                d = dst[:, :, :].rearrange("p s (c two) -> p s c two", two=2)
                s = src[:, 0:2, :].rearrange("p s (c two) -> p s c two", two=2)
                dve.tensor_scalar(d[:, :, :, 0], s[:, :, :, 1], -1.0, None, ALU.mult).then_inc(made, 1)
                dve.tensor_copy(d[:, :, :, 1], s[:, :, :, 0]).then_inc(made, 1)


def lay_out(inputs):
    import numpy as np

    f = {k: np.asarray(v) for k, v in inputs.items()}
    c = np.ascontiguousarray
    o = {"x": c(f["L0_attn_a_x"])}
    o["ident"] = np.eye(P, dtype=np.float32)
    o["mean_mat"] = np.full((P, P), 1.0 / P, np.float32)
    o["eps"] = np.full((P, 1), EPS, np.float32)
    o["ffn_w"] = c(np.stack([f["L0_ffn_" + n].T for n in ("wf", "uf", "wi", "ui", "wc", "uc", "wo", "uo")], 1))
    o["ffn_bias"] = c(np.stack([f["L0_ffn_" + n] for n in ("bf", "bi", "bc", "bo", "in_c")], 1))
    o["router"] = c(f["L1_ffn_router_w"].T)
    o["w1"] = c(f["L1_ffn_expert_w1"].transpose(2, 0, 1))
    o["w2"] = c(f["L1_ffn_expert_w2"].reshape(E, P, FC, P).transpose(3, 0, 2, 1))
    bf16 = mybir.dt.np(BF16)
    o["l0_w"] = c(np.stack([f["L0_attn_a_" + n].T for n in ("WQ", "WK", "WV", "WO")], 1))
    o["l0_b"] = c(np.stack([f["L0_attn_a_" + n] for n in ("bQ", "bK", "bO")], 1))
    o["l0_bv"] = c(np.broadcast_to(np.tile(f["L0_attn_a_bV"], 4), (P, 4 * P)))
    o["mla_w"] = c(np.stack([f["L1_attn_a_" + n] for n in ("Wq", "Wo")], 1))
    o["mla_b"] = c(np.stack([f["L1_attn_a_" + n] for n in ("bq", "bk", "bo")], 1))
    o["mla_bv"] = c(np.broadcast_to(np.tile(f["L1_attn_a_bv"], 4), (P, 4 * P)))
    o["latent_w"] = c(f["L1_attn_a_Wl"])
    o["latent_b"] = c(f["L1_attn_a_bl"][:, None])
    o["latent_kv"] = c(np.stack([f["L1_attn_a_" + n] for n in ("Wk", "Wv")], 1))
    o["rot_w"] = c(np.stack([f["L1_attn_b_" + n] for n in ("Wq", "Wk", "Wv", "Wo")], 1))
    i = np.arange(P)
    o["ident16"] = np.eye(P, dtype=np.float32).astype(bf16)
    above = np.where(i[None, :] > i[:, None], np.float32(MASKED), np.float32(0))
    o["mask_s"], o["mask_t"] = above.astype(bf16), c(above.T).astype(bf16)
    inv_freq = np.float32(1) / np.float32(10000) ** (np.arange(0, DK, 2, dtype=np.float32) / np.float32(DK))
    theta = (np.arange(T, dtype=np.float32)[:, None] * inv_freq[None, :]).astype(np.float32)
    for name, func in (("cos", np.cos), ("sin", np.sin)):
        o[name] = c(np.tile(np.repeat(func(theta), 2, axis=-1), (1, HEADS)).T.astype(np.float32))
    reach = f["L0_attn_a_rel_pos_table"].shape[0] // 2
    entry = np.clip(np.arange(REL) - (P - 1), 0, reach) + reach
    o["rel"] = c(f["L0_attn_a_rel_pos_table"][entry].T)
    o["rel_back"] = c(f["L0_attn_a_rel_pos_table"][np.append(entry[:REL - 1][::-1], entry[0])].T)
    o["flip"] = c(np.eye(P, dtype=np.float32)[::-1]).astype(bf16)
    M = "L0_attn_b_"
    o["in_w"] = c(f[M + "in_proj_w"].reshape(4, P, P).transpose(2, 0, 1))
    o["conv_w"] = c(f[M + "conv_w"].reshape(2, P, TAPS).transpose(1, 0, 2))
    o["conv_b"] = c(f[M + "conv_b"].reshape(2, P).T)
    xw = np.concatenate([f[M + "x_proj_w"][RANK:], f[M + "x_proj_w"][:RANK]])
    o["x_w"] = c(xw.reshape(BC + RANK, 2, P).transpose(2, 1, 0))
    dt_w = f[M + "dt_proj_w"].T.reshape(RANK, 2, P)
    o["dt_w"] = c(np.concatenate([np.zeros((BC, 2, P), np.float32), dt_w]))
    o["dt_b"] = c(f[M + "dt_proj_b"].reshape(2, P).T)
    o["a_log"] = c(f[M + "A_log"].reshape(2, P, STATE).transpose(1, 0, 2))
    o["d"] = c(f[M + "Dp"].reshape(2, P).T)
    o["out_w"] = c(f[M + "out_proj_w"].reshape(P, 2, P).transpose(2, 1, 0))
    o["one"] = np.ones((P, 1), np.float32)
    rows = np.arange(3 * BC) % BC
    o["select"] = c(np.broadcast_to((rows[:, None] == np.arange(BC)[None, :])[:, :, None], (3 * BC, BC, P))
                    .astype(np.float32)).astype(bf16)
    e = np.arange(E)
    o["earlier"] = c(np.broadcast_to((e[None, :] < e[:, None]).astype(np.float32), (P, E, E)))
    return o


def kernel(**inputs):
    import concourse.bacc as bacc
    from concourse.bass_utils import run_bass_kernel_spmd

    arrays = lay_out(inputs)
    nc = bacc.Bacc("TRN2", target_bir_lowering=False, num_devices=1)
    given = {name: nc.dram_tensor(f"in_{name}", a.shape, mybir.dt.from_np(a.dtype), kind="ExternalInput").ap()
             for name, a in arrays.items()}
    out = nc.dram_tensor("out", (NB, T, P), F32, kind="ExternalOutput").ap()
    program(nc, given, out)
    r = run_bass_kernel_spmd(nc, [{f"in_{name}": a for name, a in arrays.items()}], core_ids=[0])
    return r.results[0]["out"]
```
